# Optimizing a Trainium2 kernel written in Bass

```python
import numpy as np
import jax
import jax.numpy as jnp

def _softmax(x, axis=-1):
    return jax.nn.softmax(x, axis=axis)

def _gelu(x):
    return jax.nn.gelu(x, approximate=True)

def _silu(x):
    return jax.nn.silu(x)

def _sigmoid(x):
    return jax.nn.sigmoid(x)

def _layernorm(x, axis=-1, eps=1e-05):
    m = jnp.mean(x, axis=axis, keepdims=True)
    v = jnp.var(x, axis=axis, keepdims=True)
    return (x - m) / jnp.sqrt(v + eps)

def _scatter_add(tgt, idx, src, axis=0):
    return tgt.at[idx].add(src)

def _segment_sum(src, seg, n):
    return jax.ops.segment_sum(src, seg, n)
kernel_name = 'mk_xattn_seq_d1_seqx_r4_64a91f'

def setup_inputs(seed: int=0):
    np.random.seed(seed)
    _w = jnp.asarray

    def _rec_inputs():
        import jax
        import jax.numpy as jnp
        _rk = jax.random.key(seed)
        x = -0.000719 + 1.001 * jax.random.normal(jax.random.fold_in(_rk, 1), (16, 112, 320), jnp.float32)
        _lenS = 112 - jax.random.randint(jax.random.fold_in(_rk, 7), (16,), 0, max(1, 112 // 4) + 1, jnp.int32)
        _lenS2 = 375 - jax.random.randint(jax.random.fold_in(_rk, 8), (16,), 0, max(1, 375 // 4) + 1, jnp.int32)
        _ctx_2048P = jax.random.normal(jax.random.fold_in(_rk, 11), (16, 16, 512), jnp.float32)
        _ctx_2048c = jax.random.dirichlet(jax.random.fold_in(_rk, 511), 0.3 * jnp.ones((16,), jnp.float32), (16, 375))
        _ctx_2048t = jnp.einsum('bsk,bkd->bsd', _ctx_2048c, _ctx_2048P)
        _ctx_2048t = _ctx_2048t * jax.lax.rsqrt(jnp.mean(jnp.square(_ctx_2048t)) + 1e-12) * 0.953939
        ctx_2048 = 0.00257118 + 0.99863 * (_ctx_2048t + 0.3 * jax.random.normal(jax.random.fold_in(_rk, 611), (16, 375, 512), jnp.float32))
        fside_S_0 = jax.random.uniform(jax.random.fold_in(_rk, 12), (112,), jnp.float32, 0.0, 0.999706)
        return (x, ctx_2048, fside_S_0)
    x, ctx_2048, fside_S_0 = _rec_inputs()

    def _L0_xattn_setup():
        import jax, jax.numpy as jnp
        import numpy as np
        HEADS = 20
        NUM_TOKENS = 4
        IP_SCALE = 1.0
        SEM_SCALE = 0.5
        RESCALE = 1.0
        EPS = 1e-12

        def _l2norm(x, axis=-1):
            n = jnp.sqrt(jnp.sum(x * x, axis=axis, keepdims=True))
            return x / jnp.maximum(n, EPS)
        key = jax.random.key(seed)
        ks = jax.random.split(key, 10)
        B, S, C = (2, 256, 320)
        T, E = (81, 512)
        inp = {'hidden_states': jax.random.normal(ks[0], (B, S, C), jnp.float32), 'encoder_hidden_states': jax.random.normal(ks[1], (B, T, E), jnp.float32), 'spatial_mask': jax.random.uniform(ks[2], (S,), jnp.float32), 'W_q': jax.random.normal(ks[3], (C, C), jnp.float32) * C ** (-0.5), 'W_k': jax.random.normal(ks[4], (E, C), jnp.float32) * E ** (-0.5), 'W_v': jax.random.normal(ks[5], (E, C), jnp.float32) * E ** (-0.5), 'W_k_ip': jax.random.normal(ks[6], (E, C), jnp.float32) * E ** (-0.5), 'W_v_ip': jax.random.normal(ks[7], (E, C), jnp.float32) * E ** (-0.5), 'W_out': jax.random.normal(ks[8], (C, C), jnp.float32) * C ** (-0.5), 'b_out': jnp.zeros((C,), jnp.float32)}
        return inp
    _L0_xattn_all = _L0_xattn_setup()
    _L0_xattn_in = {k: v for k, v in _L0_xattn_all.items() if k in ('W_q', 'W_k', 'W_v', 'W_k_ip', 'W_v_ip', 'W_out', 'b_out')}
    del _L0_xattn_all
    return {'x': x, 'ctx_2048': ctx_2048, 'fside_S_0': fside_S_0, 'L0_xattn_W_q': _L0_xattn_in['W_q'], 'L0_xattn_W_k': _L0_xattn_in['W_k'], 'L0_xattn_W_v': _L0_xattn_in['W_v'], 'L0_xattn_W_k_ip': _L0_xattn_in['W_k_ip'], 'L0_xattn_W_v_ip': _L0_xattn_in['W_v_ip'], 'L0_xattn_W_out': _L0_xattn_in['W_out'], 'L0_xattn_b_out': _L0_xattn_in['b_out']}

def reference(x, ctx_2048, fside_S_0, L0_xattn_W_q, L0_xattn_W_k, L0_xattn_W_v, L0_xattn_W_k_ip, L0_xattn_W_v_ip, L0_xattn_W_out, L0_xattn_b_out):
    import jax
    import jax.numpy as jnp

    def _L0_xattn_ref(hidden_states, encoder_hidden_states, spatial_mask, W_q, W_k, W_v, W_k_ip, W_v_ip, W_out, b_out):
        import jax, jax.numpy as jnp
        import numpy as np
        HEADS = 20
        NUM_TOKENS = 4
        IP_SCALE = 1.0
        SEM_SCALE = 0.5
        RESCALE = 1.0
        EPS = 1e-12

        def _l2norm(x, axis=-1):
            n = jnp.sqrt(jnp.sum(x * x, axis=axis, keepdims=True))
            return x / jnp.maximum(n, EPS)
        B, S, C = hidden_states.shape
        H = HEADS
        Dh = C // H
        attn_scale = Dh ** (-0.5)
        residual = hidden_states
        text_ehs = encoder_hidden_states[:, :-NUM_TOKENS]
        ip_ehs = encoder_hidden_states[:, -NUM_TOKENS:]

        def heads(x):
            return x.reshape(B, -1, H, Dh).transpose(0, 2, 1, 3)
        q = heads(hidden_states @ W_q)
        k_t = heads(text_ehs @ W_k)
        v_t = heads(text_ehs @ W_v)
        scores_t = jnp.einsum('bhsd,bhtd->bhst', q, k_t) * attn_scale
        probs_t = jax.nn.softmax(scores_t, axis=-1)
        text_out = jnp.einsum('bhst,bhtd->bhsd', probs_t, v_t)
        text_out = text_out.transpose(0, 2, 1, 3).reshape(B, S, C)
        k_ip = heads(ip_ehs @ W_k_ip)
        v_ip = heads(ip_ehs @ W_v_ip)
        attn_scores = jnp.einsum('bhsd,bhnd->bhsn', q, k_ip) * attn_scale
        qsem = jnp.einsum('bhst,bte->bhse', probs_t, text_ehs)
        qsem = _l2norm(qsem)
        ip_n = _l2norm(ip_ehs)
        sem = jnp.einsum('bhse,bne->bhsn', qsem, ip_n)
        sem = jax.lax.stop_gradient(sem)
        fused = attn_scores + SEM_SCALE * sem
        probs_ip = jax.nn.softmax(fused, axis=-1)
        probs_ip = probs_ip * spatial_mask[None, None, :, None]
        ip_out = jnp.einsum('bhsn,bhnd->bhsd', probs_ip, v_ip)
        ip_out = ip_out.transpose(0, 2, 1, 3).reshape(B, S, C)
        out = text_out + IP_SCALE * ip_out
        out = out @ W_out + b_out
        out = out + residual
        return out / RESCALE
    x = _L0_xattn_ref(x, ctx_2048, fside_S_0, L0_xattn_W_q, L0_xattn_W_k, L0_xattn_W_v, L0_xattn_W_k_ip, L0_xattn_W_v_ip, L0_xattn_W_out, L0_xattn_b_out)
    return x

_drawn_inputs = setup_inputs


def setup_inputs(seed=0):
    import zlib

    import numpy as np

    out = dict(_drawn_inputs(seed))
    spreads = {'L0_xattn_b_out': (0.0, 0.1)}
    factors = {}
    for name, (base, spread) in spreads.items():
        noise = np.random.default_rng([zlib.crc32(name.encode()), seed]).standard_normal(out[name].shape)
        drawn = base * np.exp(spread * noise) if base else spread * noise
        out[name] = jnp.asarray(drawn.astype(out[name].dtype))
    for name, factor in factors.items():
        out[name] = (out[name] * factor).astype(out[name].dtype)
    return out
```

```python
import concourse.bass as bass
from concourse import mybir
from concourse.alu_op_type import AluOpType as ALU
from contextlib import ExitStack

F32 = mybir.dt.float32
F16 = mybir.dt.float16
ACT = mybir.ActivationFunctionType
AX = mybir.AxisListType

B, S, C = 16, 112, 320
T, E = 375, 512
NIP = 4
TX = T - NIP
H = 20
DH = C // H
P = 128
EC = E // P
CC = (C + P - 1) // P
CR = C - (CC - 1) * P
TC = T // 3
NT = 3
TROWS = [min(TC, TX - i * TC) for i in range(NT)]
NG = C // 32
HH = H // 2
VW = DH + 1 + NIP
OW = HH * 2 * VW
HALF_W = OW + HH * NIP
EPS = 1e-12
SEM_SCALE = 0.5
W_UP = 64.0
G_DOWN = 1.0 / 64.0
Q_SCALE = DH ** -0.5

NA = 14
PIECES_TEXT, PIECE_X, PIECES_K, PIECE_Q, PIECES_G, PIECES_V = (0, 1, 2), 3, (4, 5, 6), 7, (8, 9, 10), (11, 12, 13)
PREP_STEP = {0: 0, 1: 1, 2: 2, 3: 3, 4: 4, 5: 5, 6: 6, 7: 7, 9: 8, 10: 9, 12: 10, 13: 11, 15: 12, 16: 13}
NF = 4
FINISH_STEP = {8: 0, 11: 1, 14: 2, 17: 3}
SOFT_STEPS = (2, 4, 6)
FINAL_CHAIN = 11
SETUP_CHAIN = 3


def channels(j):
    return P if j < CC - 1 else CR


class Batch:

    def __init__(self, n, odd, pair):
        self.n, self.odd, self.pair = n, odd, pair

    def next(self):
        return Batch(self.n + 1, 1 - self.odd, self.pair + self.odd)

    def last(self):
        return Batch(self.n - 1, 1 - self.odd, self.pair - (1 - self.odd))


def build(nc, x, ctx, mask, w_q, w_k, w_v, w_k_ip, w_v_ip, w_out, b_out, out):
    scratch = nc.dram_tensor("v_ip_scratch", (B * NIP, C), F32, kind="Internal").ap()
    stack = ExitStack()
    with stack:
        def sb(name, shape, dt=F32):
            return stack.enter_context(nc.sbuf_tensor(name, shape, dt))

        def ps(name, shape):
            return stack.enter_context(nc.psum_tensor(name, shape, F32))

        def sem(name):
            return stack.enter_context(nc.semaphore(name))

        ident = sb("ident", [P, P])
        ones = sb("ones", [64, S])
        head_rows = sb("head_rows", [P, 2, 4])
        q_mask = sb("q_mask", [P, 2])
        mask_sb = sb("mask_sb", [S, 1])
        bias_sb = sb("bias_sb", [S, C])
        wq_sb = sb("wq_sb", [P, CC, CC * P])
        wo_sb = sb("wo_sb", [P, CC, C])
        w_raw = sb("w_raw", [P, EC, 4, C])
        w_hi = sb("w_hi", [P, EC, 2, C], F16)
        w_lo = sb("w_lo", [P, EC, 2, C], F16)
        ip_rows = sb("ip_rows", [B * NIP, E])
        ip_sq = sb("ip_sq", [B * NIP, E])
        ip_norm = sb("ip_norm", [B * NIP, 4])
        minus_half = sb("minus_half", [P, H])
        ip_diag = sb("ip_diag", [B * NIP, B * NIP])
        ip_inv = sb("ip_inv", [S, B * NIP])
        ip_T = sb("ip_T", [P, EC, B * NIP])
        kip_hi = sb("kip_hi", [P, CC, B * NIP], F16)
        kip_lo = sb("kip_lo", [P, CC, B * NIP], F16)
        kip_all = sb("kip_all", [P, NG, B * NIP], F16)
        vip_rows = sb("vip_rows", [B * NIP, C])
        vip_diag = sb("vip_diag", [H * NIP, B, C])
        ctx_sb = sb("ctx_sb", [TC, NT, E])
        x_sb = sb("x_sb", [S, CC * P])
        x_bias = [sb(f"x_bias{i}", [S, C]) for i in range(2)]
        text_hi = sb("text_hi", [P, EC, T], F16)
        text_lo = sb("text_lo", [P, EC, T], F16)
        x_T = sb("x_T", [P, CC, S])
        k_hi = sb("k_hi", [P, CC, TX], F16)
        k_lo = sb("k_lo", [P, CC, TX], F16)
        q_hi = sb("q_hi", [P, CC, 2, S], F16)
        q_lo = sb("q_lo", [P, CC, 2, S], F16)
        k_st = [sb(f"k_st{i}", [P, NG, TX], F16) for i in range(2)]
        q_st = [sb(f"q_st{i}", [P, NG, 2, S], F16) for i in range(2)]
        kip_st = [sb(f"kip_st{i}", [P, NG, NIP], F16) for i in range(2)]
        gram_hi = [sb(f"gram_hi{i}", [TC, NT, TX], F16) for i in range(2)]
        gram_lo = [sb(f"gram_lo{i}", [TC, NT, TX], F16) for i in range(2)]
        val = [sb(f"val{i}", [TC, NT, H, 2 * VW], F16) for i in range(2)]
        low = sb("low", [S, 4])
        prob = sb("prob", [S, 4, T])
        pT_hi = sb("pT_hi", [TC, 2, NT, S], F16)
        pT_lo = sb("pT_lo", [TC, 2, NT, S], F16)
        quad_junk = sb("quad_junk", [S, 2, TX])
        quad = [sb(f"quad{i}", [S, H]) for i in range(2)]
        half_sb = [sb(f"half_sb{i}", [S, 2, HALF_W]) for i in range(2)]
        vals = sb("vals", [S, H, VW])
        rsum = sb("rsum", [S, H])
        nrm = sb("nrm", [S, 4, H])
        fused = sb("fused", [S, H, NIP])
        fmax = sb("fmax", [S, 3, H])
        fexp = sb("fexp", [S, H, NIP])
        fprob = sb("fprob", [S, H, NIP])
        fprob_T = sb("fprob_T", [H * NIP, S])
        text_out = sb("text_out", [S, C])
        attn = sb("attn", [S, CC * P])
        attn_T = sb("attn_T", [P, CC, S])
        out_sb = sb("out_sb", [S, C])

        ps_score = [ps(f"ps_score{i}", [P, 512]) for i in range(2)]
        ps_pT = ps("ps_pT", [P, 512])
        ps_gram = [ps(f"ps_gram{i}", [P, 512]) for i in range(2)]
        ps_val = ps("ps_val", [P, 512])
        ps_prep = ps("ps_prep", [P, 512])
        ps_fin = ps("ps_fin", [P, 512])

        s_w = [sem(f"s_w{i}") for i in range(4)]
        s_wq, s_wo, s_ip = sem("s_wq"), sem("s_wo"), sem("s_ip")
        s_small = sem("s_small")
        s_ctx, s_x = sem("s_ctx"), sem("s_x")
        s_vip_out, s_vip_in = sem("s_vip_out"), sem("s_vip_in")
        s_kip_st = sem("s_kip_st")
        s_kst = [sem(f"s_kst{i}") for i in range(2)]
        s_qst = [sem(f"s_qst{i}") for i in range(2)]
        s_store = sem("s_store")
        s_zero, s_const, s_qmask, s_wsplit_hi, s_wsplit_lo = (sem(n) for n in ("s_zero", "s_const", "s_qmask", "s_wsplit_hi", "s_wsplit_lo"))
        s_pool_set, s_dve_set = sem("s_pool_set"), sem("s_dve_set")
        s_setup_pe, s_setup_ev = sem("s_setup_pe"), sem("s_setup_ev")
        s_prep, s_prep_hi, s_prep_lo = sem("s_prep"), sem("s_prep_hi"), sem("s_prep_lo")
        s_xbias, s_kip = sem("s_xbias"), sem("s_kip")
        s_score, s_low, s_prob = sem("s_score"), sem("s_low"), sem("s_prob")
        s_pT, s_pT_hi, s_pT_lo = sem("s_pT"), sem("s_pT_hi"), sem("s_pT_lo")
        s_gram, s_val, s_quad, s_half = sem("s_gram"), sem("s_val"), sem("s_quad"), sem("s_half")
        s_vals, s_chain, s_n2, s_rn, s_rsum = sem("s_vals"), sem("s_chain"), sem("s_n2"), sem("s_rn"), sem("s_rsum")
        s_fin_arg, s_fin_exp, s_fprob = sem("s_fin_arg"), sem("s_fin_exp"), sem("s_fprob")
        s_text_out, s_fin, s_fin_ev = sem("s_text_out"), sem("s_fin"), sem("s_fin_ev")

        block = stack.enter_context(nc.Block())

        def reached(eng, s, value):
            if not (isinstance(value, int) and value <= 0):
                eng.wait_ge(s, value)

        def all_batches(eng, body, tail):
            pairs = B // 2
            body(Batch(0, 0, 0), True, False)
            body(Batch(1, 1, 0), True, True)
            with eng.Fori(1, pairs - 1) as i:
                body(Batch(2 * i, 0, i), True, True)
                body(Batch(2 * i + 1, 1, i), True, True)
            body(Batch(B - 2, 0, pairs - 1), True, True)
            body(Batch(B - 1, 1, pairs - 1), False, True)
            tail(Batch(B, 0, pairs))

        @block.sync
        def _(sp):
            def load(a):
                reached(sp, s_prep, NA * (a.n - 1) + PIECES_TEXT[-1] + 1)
                sp.dma_start(ctx_sb[:, :, :], ctx[a.n, :, :].rearrange("(c p) e -> p c e", p=TC)).then_inc(s_ctx, 16)
                reached(sp, s_prep, NA * (a.n - 1) + PIECE_X + 1)
                reached(sp, s_xbias, a.n)
                sp.dma_start(x_sb[:, 0:C], x[a.n, :, :]).then_inc(s_x, 16)

            def restack(dst, srcs, s):
                for quad_ in range(4):
                    ng = len(range(quad_, NG, 4))
                    for term, src in enumerate(srcs):
                        sp.dma_start(dst[32 * term:32 * term + 32, quad_::4], src[32 * quad_:32 * quad_ + 32, 0:ng]).then_inc(s, 16)

            def stack_kq(a):
                reached(sp, s_score, H * (a.n - 1))
                sp.wait_ge(s_prep_lo, NA * a.n + PIECES_K[-1] + 1)
                restack(k_st[a.odd], (k_hi, k_lo, k_hi, k_lo), s_kst[a.odd])
                sp.wait_ge(s_prep_lo, NA * a.n + PIECE_Q + 1)
                restack(q_st[a.odd], (q_hi, q_hi, q_lo, q_lo), s_qst[a.odd])

            sp.dma_start(ctx_sb[:, :, :], ctx[0, :, :].rearrange("(c p) e -> p c e", p=TC)).then_inc(s_ctx, 16)
            sp.wait_ge(s_zero, 1)
            sp.dma_start(x_sb[:, 0:C], x[0, :, :]).then_inc(s_x, 16)
            for b in range(B):
                sp.dma_start(ip_rows[b * NIP:(b + 1) * NIP, :], ctx[b, TX:T, :]).then_inc(s_ip, 16)
            for i, w in enumerate((w_k, w_v, w_k_ip, w_v_ip)):
                sp.dma_start(w_raw[:, :, i, :], w.rearrange("(c p) n -> p c n", p=P)).then_inc(s_w[i], 16)
            for dst, src, s in ((wq_sb, w_q, s_wq), (wo_sb, w_out, s_wo)):
                sp.dma_start(dst[:, 0:CC - 1, 0:C], src[0:(CC - 1) * P, :].rearrange("(c p) n -> p c n", p=P)).then_inc(s, 16)
                sp.dma_start(dst[0:CR, CC - 1, 0:C], src[(CC - 1) * P:C, :]).then_inc(s, 16)
            sp.dma_start(mask_sb[:, :], mask.rearrange("(s a) -> s a", a=1)).then_inc(s_small, 16)
            sp.dma_start(bias_sb[:, :], b_out.partition_broadcast(S)).then_inc(s_small, 16)
            sp.wait_ge(s_setup_ev, 3)
            restack(kip_all, (kip_hi, kip_lo, kip_hi, kip_lo), s_kip_st)
            sp.wait_ge(s_setup_ev, 4)
            sp.dma_start(scratch[:, :], vip_rows[:, :]).then_inc(s_vip_out, 16)
            sp.wait_ge(s_vip_out, 16)
            sp.wait_ge(s_pool_set, 1)
            vip_view = scratch.rearrange("(b n) c -> n b c", n=NIP)
            for h in range(H):
                sp.dma_start(vip_diag[h * NIP:(h + 1) * NIP, :, h * DH:(h + 1) * DH],
                             vip_view[:, :, h * DH:(h + 1) * DH]).then_inc(s_vip_in, 16)
            stack_kq(Batch(0, 0, 0))

            def body(b, prepare, finishing):
                if prepare:
                    load(b.next())
                    stack_kq(b.next())

            all_batches(sp, body, lambda b: None)

        @block.gpsimd
        def _(pool):
            nc.gpsimd.memset(x_sb[:, C:CC * P], 0.0)
            nc.gpsimd.memset(wq_sb[:, :, C:CC * P], 0.0).then_inc(s_zero, 1)
            nc.gpsimd.memset(ident[:, :], 0.0)
            nc.gpsimd.memset(head_rows[:, :, :], 1.0).then_inc(s_dve_set, 1)
            pool.wait_ge(s_dve_set, 1)
            nc.gpsimd.affine_select(out=ident[:, :], in_=ident[:, :], compare_op=ALU.not_equal, fill=1.0,
                                    base=0, pattern=[[-1, P]], channel_multiplier=1).then_inc(s_const, 1)
            nc.gpsimd.affine_select(out=head_rows[:, :, :], in_=head_rows[:, :, :], compare_op=ALU.is_ge, fill=0.0,
                                    base=0, pattern=[[-DH, 2], [-2 * DH, 4]], channel_multiplier=1).then_inc(s_dve_set, 1)
            pool.wait_ge(s_dve_set, 2)
            nc.gpsimd.affine_select(out=head_rows[:, :, :], in_=head_rows[:, :, :], compare_op=ALU.is_ge, fill=0.0,
                                    base=DH - 1, pattern=[[DH, 2], [2 * DH, 4]], channel_multiplier=-1).then_inc(s_const, 1)
            nc.gpsimd.memset(minus_half[:, :], -0.5)
            nc.gpsimd.memset(ones[:, :], 1.0)
            nc.gpsimd.memset(attn[:, C:CC * P], 0.0)
            nc.gpsimd.memset(prob[:, :, TX:T], 0.0)
            for v in val:
                nc.gpsimd.memset(v[:, :, :, DH:DH + 1], 1.0)
                nc.gpsimd.memset(v[:, :, :, VW + DH:VW + DH + 1], 0.0)
            nc.gpsimd.memset(vip_diag[:, :, :], 0.0).then_inc(s_pool_set, 1)
            pool.wait_ge(s_dve_set, 3)
            pool.wait_ge(s_pool_set, 1)
            nc.gpsimd.tensor_tensor(ip_norm[:, 2:3], ip_norm[:, 1:2], minus_half[0:B * NIP, 0:1], ALU.pow).then_inc(s_pool_set, 1)

            def ready(a):
                pool.wait_ge(s_x, 16 * (a.n + 1))
                reached(pool, s_fin_ev, NF * (a.n - 1))
                nc.gpsimd.tensor_tensor(x_bias[a.odd][:, :], x_sb[:, 0:C], bias_sb[:, :], ALU.add).then_inc(s_xbias, 1)
                reached(pool, s_val, H * (a.n - 1))
                nc.gpsimd.tensor_copy(kip_st[a.odd][:, :, :], kip_all[:, :, bass.ds(a.n * NIP, NIP)]).then_inc(s_kip, 1)

            pool.wait_ge(s_small, 32)
            pool.wait_ge(s_kip_st, 16 * 16)
            ready(Batch(0, 0, 0))

            def body(b, prepare, finish):
                if finish:
                    end(b)
                if prepare:
                    ready(b.next())

            def end(b):
                f = b.last()
                hs = half_sb[f.odd]
                pool.wait_ge(s_half, 2 * f.n + 2)
                reached(pool, s_text_out, f.n)
                reached(pool, s_fin_arg, f.n)
                for half in range(2):
                    o = hs[:, half, 0:OW].rearrange("s (h w) -> s h w", w=2 * VW)
                    last = nc.gpsimd.tensor_tensor(vals[:, half * HH:(half + 1) * HH, :], o[:, :, 0:VW], o[:, :, VW:2 * VW], ALU.add)
                last.then_inc(s_vals, 1)
                pool.wait_ge(s_n2, f.n + 1)
                nc.gpsimd.tensor_tensor(nrm[:, 3, :], nrm[:, 2, :], minus_half[0:S, :], ALU.pow).then_inc(s_rn, 1)
                pool.wait_ge(s_vals, f.n + 1)
                reached(pool, s_fin_ev, NF * f.n)
                nc.gpsimd.tensor_tensor(text_out[:, :].rearrange("s (h d) -> s h d", d=DH), vals[:, :, 0:DH],
                                        rsum[:, :].unsqueeze(2).to_broadcast([S, H, DH]), ALU.mult).then_inc(s_text_out, 1)

            all_batches(pool, body, lambda b: end(b))

        @block.tensor
        def _(pe):
            def split3(dst, parts_l, parts_r, chunks):
                n, total = 0, 3 * chunks
                for c in range(chunks):
                    for a, b_ in ((0, 0), (0, 1), (1, 0)):
                        last = nc.tensor.matmul(dst, parts_l(a, c), parts_r(b_, c), start=(n == 0), stop=(n == total - 1))
                        n += 1
                return last

            text = (text_hi, text_lo)
            w = (w_hi, w_lo)

            def prep(a, k):
                reached(pe, s_prep_lo, NA * a.n + k)
                reached(pe, s_prep_hi, NA * a.n + k)
                if k in PIECES_TEXT:
                    i = k - PIECES_TEXT[0]
                    if i == 0:
                        pe.wait_ge(s_ctx, 16 * (a.n + 1))
                    for e in range(EC):
                        last = nc.tensor.transpose(ps_prep[:, e * TC:(e + 1) * TC], ctx_sb[:, i, e * P:(e + 1) * P], ident[0:TC, 0:TC])
                elif k == PIECE_X:
                    pe.wait_ge(s_x, 16 * (a.n + 1))
                    for c in range(CC):
                        last = nc.tensor.transpose(ps_prep[:, c * S:(c + 1) * S], x_sb[:, c * P:(c + 1) * P], ident[0:S, 0:S])
                elif k in PIECES_K:
                    j = k - PIECES_K[0]
                    m = channels(j)
                    last = split3(ps_prep[0:m, 0:TX], lambda h_, e: w[h_][:, e, 0, j * P:j * P + m],
                                  lambda h_, e: text[h_][:, e, 0:TX], EC)
                elif k == PIECE_Q:
                    for j in range(CC):
                        for c in range(CC):
                            last = nc.tensor.matmul(ps_prep[:, j * S:(j + 1) * S], wq_sb[0:channels(c), c, j * P:(j + 1) * P],
                                                    x_T[0:channels(c), c, :], start=(c == 0), stop=(c == CC - 1))
                elif k in PIECES_G:
                    i = k - PIECES_G[0]
                    m, n0 = TROWS[i], i * TC
                    last = split3(ps_prep[0:m, 0:T - n0], lambda h_, e: text[h_][:, e, n0:n0 + m],
                                  lambda h_, e: text[h_][:, e, n0:T], EC)
                else:
                    i = k - PIECES_V[0]
                    m, n0 = TROWS[i], i * TC
                    last = split3(ps_prep[0:m, 0:C], lambda h_, e: text[h_][:, e, n0:n0 + m],
                                  lambda h_, e: w[h_][:, e, 1, :], EC)
                last.then_inc(s_prep, 1)

            def scores(b, h):
                g = H * b.n + h
                if h == 0:
                    pe.wait_ge(s_kst[b.odd], 256 * (b.pair + 1))
                    pe.wait_ge(s_qst[b.odd], 256 * (b.pair + 1))
                reached(pe, s_prob, g - 1)
                nc.tensor.matmul(ps_score[h % 2][0:S, 0:TX], q_st[b.odd][:, h // 2, h % 2, :], k_st[b.odd][:, h // 2, :],
                                 start=True, stop=True).then_inc(s_score, 1)

            def transposes(b, h):
                g = H * b.n + h
                pe.wait_ge(s_prob, g + 1)
                reached(pe, s_pT_lo, g)
                for i in range(NT):
                    last = nc.tensor.transpose(ps_pT[0:TC, i * S:(i + 1) * S], prob[:, h % 4, i * TC:(i + 1) * TC],
                                               ident[0:S, 0:S])
                last.then_inc(s_pT, 1)

            def products(b, h):
                g = H * b.n + h
                if h == 0:
                    pe.wait_ge(s_prep_lo, NA * (b.n + 1))
                    pe.wait_ge(s_kip, b.n + 1)
                pe.wait_ge(s_pT_lo, g + 1)
                reached(pe, s_quad, g - 1)
                gh, gl, v = gram_hi[b.odd], gram_lo[b.odd], val[b.odd]
                for i in range(NT):
                    hi, lo = pT_hi[0:TROWS[i], h % 2, i, :], pT_lo[0:TROWS[i], h % 2, i, :]
                    for n, (p_, g_) in enumerate(((hi, gh), (hi, gl), (lo, gh))):
                        last = nc.tensor.matmul(ps_gram[h % 2][0:S, i * TC:TX], p_, g_[0:TROWS[i], i, i * TC:TX],
                                                start=(i == 0 and n == 0), stop=(i == NT - 1 and n == 2), skip_group_check=True)
                last.then_inc(s_gram, 1)
                hh = h % HH
                if hh == 0:
                    reached(pe, s_half, 2 * b.n + h // HH)
                for i in range(NT):
                    hi, lo = pT_hi[0:TROWS[i], h % 2, i, :], pT_lo[0:TROWS[i], h % 2, i, :]
                    o = hh * 2 * VW
                    nc.tensor.matmul(ps_val[0:S, o:o + 2 * VW], hi, v[0:TROWS[i], i, h, :], start=(i == 0), stop=False, skip_group_check=True)
                    nc.tensor.matmul(ps_val[0:S, o:o + VW], lo, v[0:TROWS[i], i, h, 0:VW], start=False, stop=(i == NT - 1), skip_group_check=True)
                nc.tensor.matmul(ps_val[0:S, OW + hh * NIP:OW + (hh + 1) * NIP], q_st[b.odd][:, h // 2, h % 2, :],
                                 kip_st[b.odd][:, h // 2, :], start=True, stop=True, skip_group_check=True).then_inc(s_val, 1)

            def finish(f, k):
                reached(pe, s_fin_ev, NF * f.n + k)
                if k == 0:
                    pe.wait_ge(s_fprob, f.n + 1)
                    last = nc.tensor.transpose(ps_fin[0:H * NIP, 0:S], fprob[:, :, :].rearrange("s h n -> s (h n)"), ident[0:S, 0:S])
                elif k == 1:
                    last = nc.tensor.matmul(ps_fin[0:S, 0:C], fprob_T[:, :], vip_diag[:, f.n, :] if isinstance(f.n, int)
                                            else vip_diag[:, bass.ds(f.n, 1), :].rearrange("p a c -> p (a c)"), start=True, stop=True)
                elif k == 2:
                    for c in range(CC):
                        last = nc.tensor.transpose(ps_fin[:, c * S:(c + 1) * S], attn[:, c * P:(c + 1) * P], ident[0:S, 0:S])
                else:
                    for c in range(CC):
                        last = nc.tensor.matmul(ps_fin[0:S, 0:C], attn_T[0:channels(c), c, :], wo_sb[0:channels(c), c, :],
                                                start=(c == 0), stop=(c == CC - 1))
                last.then_inc(s_fin, 1)

            pe.wait_ge(s_const, 1)
            pe.wait_ge(s_ip, 16 * B)
            for e in range(EC):
                last = nc.tensor.transpose(ps_prep[:, e * 64:(e + 1) * 64], ip_rows[:, e * P:(e + 1) * P], ident[0:64, 0:64])
            last.then_inc(s_setup_pe, 1)
            pe.wait_ge(s_setup_ev, 1)
            pe.wait_ge(s_w[2], 16)
            for j in range(CC):
                for e in range(EC):
                    last = nc.tensor.matmul(ps_fin[0:channels(j), j * 64:(j + 1) * 64], w_raw[:, e, 2, j * P:j * P + channels(j)],
                                            ip_T[:, e, :], start=(e == 0), stop=(e == EC - 1))
            last.then_inc(s_setup_pe, 1)
            pe.wait_ge(s_w[3], 16)
            for e in range(EC):
                last = nc.tensor.matmul(ps_val[0:64, 0:C], ip_T[:, e, :], w_raw[:, e, 3, :], start=(e == 0), stop=(e == EC - 1))
            last.then_inc(s_setup_pe, 1)
            pe.wait_ge(s_dve_set, 4)
            nc.tensor.matmul(ps_gram[0][0:S, 0:64], ones[:, :], ip_diag[:, :], start=True, stop=True).then_inc(s_setup_pe, 1)
            pe.wait_ge(s_vip_in, 16 * H)
            pe.wait_ge(s_wq, 32)
            pe.wait_ge(s_wo, 32)
            pe.wait_ge(s_wsplit_lo, 2)
            pe.wait_ge(s_setup_ev, 5)
            for k in range(NA):
                prep(Batch(0, 0, 0), k)
            first = Batch(0, 0, 0)
            scores(first, 0)
            scores(first, 1)
            transposes(first, 0)

            def body(b, prepare, finishing):
                for h in range(H):
                    if h + 2 < H:
                        scores(b, h + 2)
                    elif prepare:
                        scores(b.next(), h + 2 - H)
                    if h + 1 < H:
                        transposes(b, h + 1)
                    elif prepare:
                        transposes(b.next(), 0)
                    products(b, h)
                    if prepare and h in PREP_STEP:
                        prep(b.next(), PREP_STEP[h])
                    if finishing and h in FINISH_STEP:
                        finish(b.last(), FINISH_STEP[h])

            def tail(b):
                for k in range(NF):
                    finish(b.last(), k)

            all_batches(pe, body, tail)

        @block.scalar
        def _(act):
            def prep_hi(a, k):
                act.wait_ge(s_prep, NA * a.n + k + 1)
                if k in PIECES_TEXT:
                    i = k - PIECES_TEXT[0]
                    last = nc.scalar.activation(text_hi[:, :, i * TC:(i + 1) * TC],
                                                ps_prep[:, 0:EC * TC].rearrange("p (e t) -> p e t", t=TC), ACT.Copy)
                elif k == PIECE_X:
                    last = nc.scalar.activation(x_T[:, 0:CC - 1, :].rearrange("p c s -> p (c s)"), ps_prep[:, 0:(CC - 1) * S], ACT.Copy)
                elif k in PIECES_K:
                    j = k - PIECES_K[0]
                    if j == 0:
                        reached(act, s_kst[1 - a.odd], 256 * (a.last().pair + 1))
                    m = channels(j)
                    last = nc.scalar.activation(k_hi[0:m, j, :], ps_prep[0:m, 0:TX], ACT.Copy, scale=1.0 / W_UP)
                elif k == PIECE_Q:
                    reached(act, s_qst[1 - a.odd], 256 * (a.last().pair + 1))
                    for e in range(2):
                        last = nc.scalar.activation(q_hi[:, :, e, :], ps_prep[:, 0:CC * S].rearrange("p (c s) -> p c s", s=S),
                                                    ACT.Copy, scale=q_mask[:, e:e + 1])
                elif k in PIECES_G:
                    i = k - PIECES_G[0]
                    m, n0 = TROWS[i], i * TC
                    if i == 0:
                        reached(act, s_val, H * (a.n - 1))
                    g = gram_hi[a.odd]
                    nc.scalar.activation(g[0:m, i, n0:n0 + m], ps_prep[0:m, 0:m], ACT.Copy, scale=G_DOWN)
                    if i < NT - 1:
                        nc.scalar.activation(g[0:m, i, n0 + m:TX], ps_prep[0:m, m:TX - n0], ACT.Copy, scale=2 * G_DOWN)
                    last = nc.scalar.activation(val[a.odd][0:m, i, :, DH + 1:VW],
                                                ps_prep[0:m, TX - n0:T - n0].unsqueeze(1).to_broadcast([m, H, NIP]), ACT.Copy, scale=G_DOWN)
                else:
                    i = k - PIECES_V[0]
                    m = TROWS[i]
                    last = nc.scalar.activation(val[a.odd][0:m, i, :, 0:DH], ps_prep[0:m, 0:C].rearrange("p (h d) -> p h d", d=DH),
                                                ACT.Copy, scale=1.0 / W_UP)
                last.then_inc(s_prep_hi, 1)

            def exps(b, h):
                g = H * b.n + h
                act.wait_ge(s_low, g + 1)
                reached(act, s_quad, g - 3)
                nc.scalar.activation(prob[:, h % 4, 0:TX], ps_score[h % 2][0:S, 0:TX], ACT.Exp, bias=low[:, h % 4:h % 4 + 1],
                                     scale=-1.0).then_inc(s_prob, 1)

            def probs_hi(b, h):
                g = H * b.n + h
                act.wait_ge(s_pT, g + 1)
                reached(act, s_val, g - 1)
                nc.scalar.activation(pT_hi[:, h % 2, :, :].rearrange("p c s -> p (c s)"), ps_pT[0:TC, 0:NT * S], ACT.Copy).then_inc(s_pT_hi, 1)

            def half_out(b, half):
                act.wait_ge(s_val, H * b.n + (half + 1) * HH)
                if half == 0:
                    reached(act, s_text_out, b.n - 1)
                    reached(act, s_fin_arg, b.n - 1)
                nc.scalar.activation(half_sb[b.odd][:, half, :], ps_val[0:S, 0:HALF_W], ACT.Copy).then_inc(s_half, 1)

            def fin_exp(f):
                act.wait_ge(s_fin_arg, f.n + 1)
                reached(act, s_fprob, f.n)
                nc.scalar.activation(fexp[:, :, :], fused[:, :, :], ACT.Exp).then_inc(s_fin_exp, 1)

            def store(f):
                act.wait_ge(s_fin_ev, NF * (f.n + 1))
                act.dma_start(out[f.n, :, :], out_sb[:, :]).then_inc(s_store, 16)

            for i in range(2):
                act.wait_ge(s_w[i], 16)
                nc.scalar.activation(w_hi[:, :, i, :], w_raw[:, :, i, :], ACT.Copy, scale=W_UP).then_inc(s_wsplit_hi, 1)
            act.wait_ge(s_qmask, 1)
            first = Batch(0, 0, 0)
            for k in range(NA):
                prep_hi(first, k)
            exps(first, 0)
            probs_hi(first, 0)
            exps(first, 1)

            def body(b, prepare, finishing):
                for h in range(H):
                    if h + 1 < H:
                        probs_hi(b, h + 1)
                    elif prepare:
                        probs_hi(b.next(), 0)
                    if h + 2 < H:
                        exps(b, h + 2)
                    elif prepare:
                        exps(b.next(), h + 2 - H)
                    if h % HH == HH - 1:
                        half_out(b, h // HH)
                    if prepare and h in PREP_STEP:
                        prep_hi(b.next(), PREP_STEP[h])
                    if finishing and h == SOFT_STEPS[1] + 1:
                        fin_exp(b.last())
                    if finishing and h == H - 2:
                        store(b.last())

            def tail(b):
                fin_exp(b.last())
                store(b.last())
                act.wait_ge(s_store, 16 * B)

            all_batches(act, body, tail)

        @block.vector
        def _(dve):
            def low_part(out_, psum, scale, hi):
                return nc.vector.scalar_tensor_tensor(out=out_, in0=psum, scalar=scale, in1=hi, op0=ALU.mult, op1=ALU.subtract)

            def prep_lo(a, k):
                dve.wait_ge(s_prep_hi, NA * a.n + k + 1)
                if k in PIECES_TEXT:
                    i = k - PIECES_TEXT[0]
                    last = nc.vector.tensor_tensor(text_lo[:, :, i * TC:(i + 1) * TC],
                                                   ps_prep[:, 0:EC * TC].rearrange("p (e t) -> p e t", t=TC),
                                                   text_hi[:, :, i * TC:(i + 1) * TC], ALU.subtract)
                elif k == PIECE_X:
                    last = nc.vector.tensor_copy(x_T[:, CC - 1, :], ps_prep[:, (CC - 1) * S:CC * S])
                elif k in PIECES_K:
                    j = k - PIECES_K[0]
                    m = channels(j)
                    if j == 0:
                        reached(dve, s_kst[1 - a.odd], 256 * (a.last().pair + 1))
                    last = low_part(k_lo[0:m, j, :], ps_prep[0:m, 0:TX], 1.0 / W_UP, k_hi[0:m, j, :])
                elif k == PIECE_Q:
                    reached(dve, s_qst[1 - a.odd], 256 * (a.last().pair + 1))
                    for e in range(2):
                        last = low_part(q_lo[:, :, e, :], ps_prep[:, 0:CC * S].rearrange("p (c s) -> p c s", s=S),
                                        q_mask[:, e:e + 1], q_hi[:, :, e, :])
                elif k in PIECES_G:
                    i = k - PIECES_G[0]
                    m, n0 = TROWS[i], i * TC
                    if i == 0:
                        reached(dve, s_val, H * (a.n - 1))
                    g, gl, v = gram_hi[a.odd], gram_lo[a.odd], val[a.odd]
                    low_part(gl[0:m, i, n0:n0 + m], ps_prep[0:m, 0:m], G_DOWN, g[0:m, i, n0:n0 + m])
                    if i < NT - 1:
                        low_part(gl[0:m, i, n0 + m:TX], ps_prep[0:m, m:TX - n0], 2 * G_DOWN, g[0:m, i, n0 + m:TX])
                    last = low_part(v[0:m, i, :, VW + DH + 1:2 * VW],
                                    ps_prep[0:m, TX - n0:T - n0].unsqueeze(1).to_broadcast([m, H, NIP]), G_DOWN, v[0:m, i, :, DH + 1:VW])
                else:
                    i = k - PIECES_V[0]
                    m = TROWS[i]
                    last = low_part(val[a.odd][0:m, i, :, VW:VW + DH], ps_prep[0:m, 0:C].rearrange("p (h d) -> p h d", d=DH),
                                    1.0 / W_UP, val[a.odd][0:m, i, :, 0:DH])
                last.then_inc(s_prep_lo, 1)

            def minimum(b, h):
                g = H * b.n + h
                dve.wait_ge(s_score, g + 1)
                reached(dve, s_prob, g - 3)
                nc.vector.tensor_reduce(low[:, h % 4:h % 4 + 1], ps_score[h % 2][0:S, 0:TX], AX.X, ALU.min).then_inc(s_low, 1)

            def probs_lo(b, h):
                g = H * b.n + h
                dve.wait_ge(s_pT_hi, g + 1)
                nc.vector.tensor_tensor(pT_lo[:, h % 2, :, :].rearrange("p c s -> p (c s)"), ps_pT[0:TC, 0:NT * S],
                                        pT_hi[:, h % 2, :, :].rearrange("p c s -> p (c s)"), ALU.subtract).then_inc(s_pT_lo, 1)

            def quadratic(b, h):
                g = H * b.n + h
                dve.wait_ge(s_gram, g + 1)
                nc.vector.tensor_tensor_reduce(out=quad_junk[:, h % 2, :], in0=ps_gram[h % 2][0:S, 0:TX], in1=prob[:, h % 4, 0:TX], scale=1.0,
                                               scalar=0.0, op0=ALU.mult, op1=ALU.add,
                                               accum_out=quad[b.odd][:, h:h + 1]).then_inc(s_quad, 1)

            def chain(f, k, ins):
                ins.then_inc(s_chain, 1)
                dve.wait_ge(s_chain, FINAL_CHAIN * f.n + SETUP_CHAIN + k + 1)

            def soft(f, part):
                def over_ip(v):
                    return v.unsqueeze(2).to_broadcast([S, H, NIP])

                if part == 0:
                    dve.wait_ge(s_vals, f.n + 1)
                    dve.wait_ge(s_quad, H * (f.n + 1))
                    reached(dve, s_text_out, f.n)
                    chain(f, 0, nc.vector.reciprocal(rsum[:, :], vals[:, :, DH]))
                    chain(f, 1, nc.vector.tensor_tensor(nrm[:, 0, :], quad[f.odd][:, :], rsum[:, :], ALU.mult))
                    chain(f, 2, nc.vector.tensor_tensor(nrm[:, 1, :], nrm[:, 0, :], rsum[:, :], ALU.mult))
                    nc.vector.tensor_scalar(nrm[:, 2, :], nrm[:, 1, :], 1.0 / G_DOWN, EPS * EPS, ALU.mult, ALU.max).then_inc(s_n2, 1)
                elif part == 1:
                    dve.wait_ge(s_rn, f.n + 1)
                    reached(dve, s_fin_exp, f.n)
                    chain(f, 3, nc.vector.tensor_tensor(nrm[:, 0, :], nrm[:, 3, :], rsum[:, :], ALU.mult))
                    chain(f, 4, nc.vector.tensor_tensor(fused[:, :, :], vals[:, :, DH + 1:VW], over_ip(nrm[:, 0, :]), ALU.mult))
                    inv = ip_inv[:, bass.ds(f.n * NIP, NIP)].unsqueeze(1).to_broadcast([S, H, NIP])
                    chain(f, 5, nc.vector.tensor_tensor(fused[:, :, :], fused[:, :, :], inv, ALU.mult))
                    ip_score = half_sb[f.odd][:, :, OW:HALF_W].rearrange("s a (h n) -> s a h n", n=NIP)
                    halves = fused[:, :, :].rearrange("s (a h) n -> s a h n", a=2)
                    chain(f, 6, nc.vector.tensor_tensor(halves, halves, ip_score, ALU.subtract))
                    chain(f, 7, nc.vector.tensor_reduce(fmax[:, 0, :], fused[:, :, :], AX.X, ALU.max))
                    nc.vector.tensor_tensor(fused[:, :, :], fused[:, :, :], over_ip(fmax[:, 0, :]), ALU.subtract).then_inc(s_fin_arg, 1)
                else:
                    dve.wait_ge(s_fin_exp, f.n + 1)
                    reached(dve, s_fin, NF * f.n)
                    chain(f, 8, nc.vector.tensor_reduce(fmax[:, 1, :], fexp[:, :, :], AX.X, ALU.add))
                    chain(f, 9, nc.vector.reciprocal(fmax[:, 2, :], fmax[:, 1, :]))
                    chain(f, 10, nc.vector.tensor_scalar(fmax[:, 1, :], fmax[:, 2, :], mask_sb[:, 0:1], None, ALU.mult))
                    nc.vector.tensor_tensor(fprob[:, :, :], fexp[:, :, :], over_ip(fmax[:, 1, :]), ALU.mult).then_inc(s_fprob, 1)

            def finish(f, k):
                dve.wait_ge(s_fin, NF * f.n + k + 1)
                if k == 0:
                    last = nc.vector.tensor_copy(fprob_T[:, :], ps_fin[0:H * NIP, 0:S])
                elif k == 1:
                    dve.wait_ge(s_text_out, f.n + 1)
                    last = nc.vector.tensor_tensor(attn[:, 0:C], ps_fin[0:S, 0:C], text_out[:, :], ALU.add)
                elif k == 2:
                    last = nc.vector.tensor_copy(attn_T[:, :, :].rearrange("p c s -> p (c s)"), ps_fin[:, 0:CC * S])
                else:
                    reached(dve, s_store, 16 * f.n)
                    last = nc.vector.tensor_tensor(out_sb[:, :], ps_fin[0:S, 0:C], x_bias[f.odd][:, :], ALU.add)
                last.then_inc(s_fin_ev, 1)

            dve.wait_ge(s_const, 2)
            nc.vector.tensor_reduce(q_mask[:, :], head_rows[:, :, :], AX.X, ALU.add).then_inc(s_chain, 1)
            dve.wait_ge(s_chain, 1)
            nc.vector.tensor_scalar(q_mask[:, :], q_mask[:, :], -Q_SCALE, None, ALU.mult).then_inc(s_qmask, 1)
            dve.wait_ge(s_ip, 16 * B)
            nc.vector.tensor_tensor_reduce(out=ip_sq[:, :], in0=ip_rows[:, :], in1=ip_rows[:, :], scale=1.0, scalar=0.0,
                                           op0=ALU.mult, op1=ALU.add, accum_out=ip_norm[:, 0:1]).then_inc(s_chain, 1)
            dve.wait_ge(s_chain, 2)
            nc.vector.tensor_scalar(ip_norm[:, 1:2], ip_norm[:, 0:1], EPS * EPS, None, ALU.max).then_inc(s_dve_set, 1)
            dve.wait_ge(s_setup_pe, 1)
            nc.vector.tensor_copy(ip_T[:, :, :].rearrange("p e t -> p (e t)"), ps_prep[:, 0:EC * 64]).then_inc(s_setup_ev, 1)
            dve.wait_ge(s_pool_set, 2)
            nc.vector.tensor_scalar(ip_norm[:, 3:4], ip_norm[:, 2:3], SEM_SCALE / G_DOWN, None, ALU.mult).then_inc(s_chain, 1)
            dve.wait_ge(s_chain, 3)
            nc.vector.tensor_scalar(ip_diag[:, :], ident[0:64, 0:64], ip_norm[:, 3:4], None, ALU.mult).then_inc(s_dve_set, 1)
            dve.wait_ge(s_setup_pe, 2)
            for m, c0, c1 in ((P, 0, CC - 1), (CR, CC - 1, CC)):
                last = nc.vector.tensor_copy(kip_hi[0:m, c0:c1, :].rearrange("p c t -> p (c t)"), ps_fin[0:m, c0 * 64:c1 * 64])
            last.then_inc(s_setup_ev, 1)
            dve.wait_ge(s_setup_ev, 2)
            for m, c0, c1 in ((P, 0, CC - 1), (CR, CC - 1, CC)):
                last = nc.vector.tensor_tensor(kip_lo[0:m, c0:c1, :].rearrange("p c t -> p (c t)"), ps_fin[0:m, c0 * 64:c1 * 64],
                                               kip_hi[0:m, c0:c1, :].rearrange("p c t -> p (c t)"), ALU.subtract)
            last.then_inc(s_setup_ev, 1)
            dve.wait_ge(s_setup_pe, 3)
            nc.vector.tensor_copy(vip_rows[:, :], ps_val[0:64, 0:C]).then_inc(s_setup_ev, 1)
            dve.wait_ge(s_setup_pe, 4)
            nc.vector.tensor_copy(ip_inv[:, :], ps_gram[0][0:S, 0:64]).then_inc(s_setup_ev, 1)
            for i in range(2):
                dve.wait_ge(s_wsplit_hi, i + 1)
                low_part(w_lo[:, :, i, :], w_raw[:, :, i, :], W_UP, w_hi[:, :, i, :]).then_inc(s_wsplit_lo, 1)
            dve.wait_ge(s_small, 32)
            first = Batch(0, 0, 0)
            for k in range(NA):
                prep_lo(first, k)
            minimum(first, 0)
            minimum(first, 1)
            probs_lo(first, 0)

            def body(b, prepare, finishing):
                for h in range(H):
                    if h + 2 < H:
                        minimum(b, h + 2)
                    elif prepare:
                        minimum(b.next(), h + 2 - H)
                    if h + 1 < H:
                        probs_lo(b, h + 1)
                    elif prepare:
                        probs_lo(b.next(), 0)
                    quadratic(b, h)
                    if prepare and h in PREP_STEP:
                        prep_lo(b.next(), PREP_STEP[h])
                    if finishing and h in SOFT_STEPS:
                        soft(b.last(), SOFT_STEPS.index(h))
                    if finishing and h in FINISH_STEP:
                        finish(b.last(), FINISH_STEP[h])

            def tail(b):
                for part in range(3):
                    soft(b.last(), part)
                for k in range(NF):
                    finish(b.last(), k)

            all_batches(dve, body, tail)


_INS = ['x', 'ctx_2048', 'fside_S_0', 'L0_xattn_W_q', 'L0_xattn_W_k', 'L0_xattn_W_v', 'L0_xattn_W_k_ip', 'L0_xattn_W_v_ip',
        'L0_xattn_W_out', 'L0_xattn_b_out']


def kernel(**inputs):
    import numpy as np
    import concourse.bacc as bacc
    from concourse.bass_utils import run_bass_kernel_spmd

    nc = bacc.Bacc("TRN2", target_bir_lowering=False, num_devices=1)
    arrays, args = {}, []
    for name in _INS:
        a = np.ascontiguousarray(inputs[name])
        arrays[f"in_{name}"] = a
        args.append(nc.dram_tensor(f"in_{name}", a.shape, mybir.dt.from_np(a.dtype), kind="ExternalInput").ap())
    args.append(nc.dram_tensor("out_0", (B, S, C), F32, kind="ExternalOutput").ap())
    build(nc, *args)
    r = run_bass_kernel_spmd(nc, [arrays], core_ids=[0])
    return r.results[0]["out_0"]
```

```python
import concourse.bass as bass
from concourse import mybir
from concourse.alu_op_type import AluOpType as ALU
from contextlib import ExitStack

F32 = mybir.dt.float32
F16 = mybir.dt.float16
ACT = mybir.ActivationFunctionType
AX = mybir.AxisListType

B, S, C = 16, 112, 320
T, E = 375, 512
NIP = 4
TX = T - NIP
H = 20
DH = C // H
P = 128
EC = E // P
CC = (C + P - 1) // P
CR = C - (CC - 1) * P
TC = T // 3
NT = 3
TROWS = [min(TC, TX - i * TC) for i in range(NT)]
NG = C // 32
HH = H // 2
VW = DH + 1 + NIP
OW = HH * 2 * VW
HALF_W = OW + HH * NIP
EPS = 1e-12
SEM_SCALE = 0.5
W_UP = 64.0
G_DOWN = 1.0 / 64.0
Q_SCALE = DH ** -0.5

NA = 15
PIECES_TEXT, PIECE_X, PIECES_K, PIECE_Q = (0, 1, 2), 3, (4, 5, 6), 7
PIECES_G, PIECE_GT, PIECES_V = (8, 9, 10), 11, (12, 13, 14)
NF = 4
FINISH_STEP = {9: 0, 12: 1, 14: 2, 17: 3}
PREP_STEP = {h: k for k, h in enumerate([h for h in range(19) if h not in FINISH_STEP])}
VALS_STEP, NORM_STEP = 0, 1
POW_STEPS = (2, 3, 4, 5)
ARG_STEP, EXP_STEP, PROB_STEP = 6, 7, 8
TEXT_OUT_STEP = 8
K_IP_STEP, RESIDUAL_STEP = 10, 19
POW_HEADS = H // len(POW_STEPS)
SP_ = P
TP = 3 * P
FINAL_CHAIN = 11
SETUP_CHAIN = 3


def channels(j):
    return P if j < CC - 1 else CR


class Batch:

    def __init__(self, n, odd, pair):
        self.n, self.odd, self.pair = n, odd, pair

    def next(self):
        return Batch(self.n + 1, 1 - self.odd, self.pair + self.odd)

    def last(self):
        return Batch(self.n - 1, 1 - self.odd, self.pair - (1 - self.odd))


def build(nc, x, ctx, mask, w_q, w_k, w_v, w_k_ip, w_v_ip, w_out, b_out, out):
    scratch = nc.dram_tensor("v_ip_scratch", (B * NIP, C), F32, kind="Internal").ap()
    stack = ExitStack()
    with stack:
        def sb(name, shape, dt=F32):
            return stack.enter_context(nc.sbuf_tensor(name, shape, dt))

        def ps(name, shape):
            return stack.enter_context(nc.psum_tensor(name, shape, F32))

        def sem(name):
            return stack.enter_context(nc.semaphore(name))

        ident = sb("ident", [P, P])
        ident_16 = sb("ident_16", [P, P], F16)
        ones = sb("ones", [64, S])
        head_rows = sb("head_rows", [P, 2, 4])
        q_mask = sb("q_mask", [P, 2])
        mask_sb = sb("mask_sb", [S, 1])
        bias_sb = sb("bias_sb", [S, C])
        wq_sb = sb("wq_sb", [P, CC, CC * P])
        wo_sb = sb("wo_sb", [P, CC, C])
        w_raw = sb("w_raw", [P, EC, 4, C])
        w_hi = sb("w_hi", [P, EC, 2, C], F16)
        w_lo = sb("w_lo", [P, EC, 2, C], F16)
        ip_rows = sb("ip_rows", [B * NIP, E])
        ip_sq = sb("ip_sq", [B * NIP, E])
        ip_norm = sb("ip_norm", [B * NIP, 4])
        minus_half = sb("minus_half", [P, H])
        ip_diag = sb("ip_diag", [B * NIP, B * NIP])
        ip_inv = sb("ip_inv", [S, B * NIP])
        ip_T = sb("ip_T", [P, EC, B * NIP])
        kip_hi = sb("kip_hi", [P, CC, B * NIP], F16)
        kip_lo = sb("kip_lo", [P, CC, B * NIP], F16)
        kip_all = sb("kip_all", [P, NG, B * NIP], F16)
        vip_rows = sb("vip_rows", [B * NIP, C])
        vip_diag = sb("vip_diag", [H * NIP, B, C])
        ctx_sb = sb("ctx_sb", [TC, NT, E])
        x_sb = sb("x_sb", [S, CC * P])
        x_bias = [sb(f"x_bias{i}", [S, C]) for i in range(2)]
        text_hi = sb("text_hi", [P, EC, TP], F16)
        text_lo = sb("text_lo", [P, EC, TP], F16)
        x_T = sb("x_T", [P, CC, S])
        k_hi = sb("k_hi", [P, CC, TX], F16)
        k_lo = sb("k_lo", [P, CC, TX], F16)
        q_hi = sb("q_hi", [P, CC, 2, SP_], F16)
        q_lo = sb("q_lo", [P, CC, 2, SP_], F16)
        k_st = [sb(f"k_st{i}", [P, NG, TX], F16) for i in range(2)]
        q_st = [sb(f"q_st{i}", [P, NG, 2, SP_], F16) for i in range(2)]
        kip_st = [sb(f"kip_st{i}", [P, NG, NIP], F16) for i in range(2)]
        gram_hi = [sb(f"gram_hi{i}", [TC, NT, TX], F16) for i in range(2)]
        gram_lo = [sb(f"gram_lo{i}", [TC, NT, TX], F16) for i in range(2)]
        gram_2hi = sb("gram_2hi", [TC, 2, TX], F16)
        val = [sb(f"val{i}", [TC, NT, H, 2 * VW], F16) for i in range(2)]
        low = sb("low", [S, 4])
        prob = sb("prob", [S, 4, T])
        pT_hi = sb("pT_hi", [TC, 2, NT, SP_], F16)
        pT_lo = sb("pT_lo", [TC, 2, NT, SP_], F16)
        prob_16 = sb("prob_16", [S, 2, TX], F16)
        dual = sb("dual", [S, 2, TX])
        quad_junk = sb("quad_junk", [S, 2, TX])
        quad = [sb(f"quad{i}", [S, H]) for i in range(2)]
        half_sb = [sb(f"half_sb{i}", [S, 2, HALF_W]) for i in range(2)]
        vals = sb("vals", [S, H, VW])
        rsum = sb("rsum", [S, H])
        nrm = sb("nrm", [S, 4, H])
        fused = sb("fused", [S, H, NIP])
        fmax = sb("fmax", [S, 3, H])
        fexp = sb("fexp", [S, H, NIP])
        fprob = sb("fprob", [S, H, NIP])
        fprob_T = sb("fprob_T", [H * NIP, S])
        text_out = sb("text_out", [S, C])
        attn = sb("attn", [S, CC * P])
        attn_T = sb("attn_T", [P, CC, S])
        out_sb = sb("out_sb", [S, C])

        ps_score = [ps(f"ps_score{i}", [P, 512]) for i in range(2)]
        ps_pT = ps("ps_pT", [P, 512])
        ps_gram = [ps(f"ps_gram{i}", [P, 512]) for i in range(2)]
        ps_val = ps("ps_val", [P, 512])
        ps_prep = ps("ps_prep", [P, 512])
        ps_fin = ps("ps_fin", [P, 512])

        s_w = [sem(f"s_w{i}") for i in range(4)]
        s_wq, s_wo, s_ip = sem("s_wq"), sem("s_wo"), sem("s_ip")
        s_small = sem("s_small")
        s_ctx, s_x = sem("s_ctx"), sem("s_x")
        s_ctx0 = [sem(f"s_ctx0_{i}") for i in range(NT)]
        s_vip_out, s_vip_in = sem("s_vip_out"), sem("s_vip_in")
        s_kip_st = sem("s_kip_st")
        s_kst = [sem(f"s_kst{i}") for i in range(2)]
        s_qst = [sem(f"s_qst{i}") for i in range(2)]
        s_store = sem("s_store")
        s_zero, s_const, s_qmask, s_wsplit_hi, s_wsplit_lo = (sem(n) for n in ("s_zero", "s_const", "s_qmask", "s_wsplit_hi", "s_wsplit_lo"))
        s_pool_set, s_fill, s_ipsq, s_ipdiag = sem("s_pool_set"), sem("s_fill"), sem("s_ipsq"), sem("s_ipdiag")
        s_setup_pe, s_setup_ev = sem("s_setup_pe"), sem("s_setup_ev")
        s_prep, s_prep_hi, s_prep_lo = sem("s_prep"), sem("s_prep_hi"), sem("s_prep_lo")
        s_xbias, s_kip = sem("s_xbias"), sem("s_kip")
        s_score, s_low, s_prob = sem("s_score"), sem("s_low"), sem("s_prob")
        s_pT, s_pT_hi, s_pT_lo = sem("s_pT"), sem("s_pT_hi"), sem("s_pT_lo")
        s_prob_16, s_dual = sem("s_prob_16"), sem("s_dual")
        s_gram, s_val, s_quad, s_half = sem("s_gram"), sem("s_val"), sem("s_quad"), sem("s_half")
        s_vals, s_chain, s_n2, s_rn, s_rsum = sem("s_vals"), sem("s_chain"), sem("s_n2"), sem("s_rn"), sem("s_rsum")
        s_fin_arg, s_fin_exp, s_fprob = sem("s_fin_arg"), sem("s_fin_exp"), sem("s_fprob")
        s_text_out, s_fin, s_fin_ev = sem("s_text_out"), sem("s_fin"), sem("s_fin_ev")

        SETUP_BANKS = (ps_prep, ps_gram[0], ps_gram[1])

        block = stack.enter_context(nc.Block())

        def reached(eng, s, value):
            if not (isinstance(value, int) and value <= 0):
                eng.wait_ge(s, value)

        def all_batches(eng, body, tail):
            pairs = B // 2
            body(Batch(0, 0, 0), True, False)
            body(Batch(1, 1, 0), True, True)
            with eng.Fori(1, pairs - 1) as i:
                body(Batch(2 * i, 0, i), True, True)
                body(Batch(2 * i + 1, 1, i), True, True)
            body(Batch(B - 2, 0, pairs - 1), True, True)
            body(Batch(B - 1, 1, pairs - 1), False, True)
            tail(Batch(B, 0, pairs))

        def load_rows(eng, dst, src, s):
            eng.dma_start(dst[:, 0:CC - 1, 0:C], src[0:(CC - 1) * P, :].rearrange("(c p) n -> p c n", p=P)).then_inc(s, 16)
            eng.dma_start(dst[0:CR, CC - 1, 0:C], src[(CC - 1) * P:C, :]).then_inc(s, 16)

        @block.sync
        def _(sp):
            def load(a):
                reached(sp, s_prep, NA * (a.n - 1) + PIECES_TEXT[-1] + 1)
                sp.dma_start(ctx_sb[:, :, :], ctx[a.n, :, :].rearrange("(c p) e -> p c e", p=TC)).then_inc(s_ctx, 16)
                reached(sp, s_prep, NA * (a.n - 1) + PIECE_X + 1)
                reached(sp, s_xbias, a.n)
                sp.dma_start(x_sb[:, 0:C], x[a.n, :, :]).then_inc(s_x, 16)

            def restack(dst, srcs, s):
                for quad_ in range(4):
                    ng = len(range(quad_, NG, 4))
                    for term, src in enumerate(srcs):
                        sp.dma_start(dst[32 * term:32 * term + 32, quad_::4], src[32 * quad_:32 * quad_ + 32, 0:ng]).then_inc(s, 16)

            def stack_kq(a):
                reached(sp, s_score, H * (a.n - 1))
                sp.wait_ge(s_prep_lo, NA * a.n + PIECES_K[-1] + 1)
                restack(k_st[a.odd], (k_hi, k_lo, k_hi, k_lo), s_kst[a.odd])
                sp.wait_ge(s_prep_lo, NA * a.n + PIECE_Q + 1)
                restack(q_st[a.odd], (q_hi, q_hi, q_lo, q_lo), s_qst[a.odd])

            def spread_v_ip():
                sp.wait_ge(s_setup_ev, 4)
                sp.dma_start(scratch[:, :], vip_rows[:, :]).then_inc(s_vip_out, 16)
                sp.wait_ge(s_vip_out, 16)
                sp.wait_ge(s_pool_set, 1)
                vip_view = scratch.rearrange("(b n) c -> n b c", n=NIP)
                for h in range(H):
                    sp.dma_start(vip_diag[h * NIP:(h + 1) * NIP, :, h * DH:(h + 1) * DH],
                                 vip_view[:, :, h * DH:(h + 1) * DH]).then_inc(s_vip_in, 16)

            for c in range(NT):
                sp.dma_start(ctx_sb[:, c, :], ctx[0, c * TC:(c + 1) * TC, :]).then_inc(s_ctx0[c], 16)
            sp.wait_ge(s_zero, 1)
            sp.dma_start(x_sb[:, 0:C], x[0, :, :]).then_inc(s_x, 16)
            for b in range(B):
                sp.dma_start(ip_rows[b * NIP:(b + 1) * NIP, :], ctx[b, TX:T, :]).then_inc(s_ip, 16)
            sp.dma_start(bias_sb[:, :], b_out.partition_broadcast(S)).then_inc(s_small, 16)
            sp.dma_start(mask_sb[:, :], mask.rearrange("(s a) -> s a", a=1)).then_inc(s_small, 16)
            load_rows(sp, wo_sb, w_out, s_wo)
            sp.wait_ge(s_const, 3)
            stack_kq(Batch(0, 0, 0))
            sp.wait_ge(s_setup_ev, 3)
            restack(kip_all, (kip_hi, kip_lo, kip_hi, kip_lo), s_kip_st)

            def body(b, prepare, finishing):
                if prepare:
                    load(b.next())
                    if isinstance(b.n, int) and b.n == 0:
                        spread_v_ip()
                    stack_kq(b.next())

            all_batches(sp, body, lambda b: None)

        @block.gpsimd
        def _(pool):
            nc.gpsimd.memset(x_sb[:, C:CC * P], 0.0)
            nc.gpsimd.memset(wq_sb[:, :, C:CC * P], 0.0).then_inc(s_zero, 1)
            nc.gpsimd.memset(ident[:, :], 0.0)
            nc.gpsimd.memset(head_rows[:, :, :], 1.0).then_inc(s_fill, 1)
            pool.wait_ge(s_fill, 1)
            nc.gpsimd.affine_select(out=ident[:, :], in_=ident[:, :], compare_op=ALU.not_equal, fill=1.0,
                                    base=0, pattern=[[-1, P]], channel_multiplier=1).then_inc(s_const, 1)
            nc.gpsimd.affine_select(out=head_rows[:, :, :], in_=head_rows[:, :, :], compare_op=ALU.is_ge, fill=0.0,
                                    base=0, pattern=[[-DH, 2], [-2 * DH, 4]], channel_multiplier=1).then_inc(s_fill, 1)
            pool.wait_ge(s_fill, 2)
            nc.gpsimd.affine_select(out=head_rows[:, :, :], in_=head_rows[:, :, :], compare_op=ALU.is_ge, fill=0.0,
                                    base=DH - 1, pattern=[[DH, 2], [2 * DH, 4]], channel_multiplier=-1).then_inc(s_const, 1)
            for t_ in (text_hi, text_lo):
                nc.gpsimd.memset(t_[:, :, T:TP], 0.0)
            for t_ in (q_hi, q_lo, pT_hi, pT_lo):
                nc.gpsimd.memset(t_[:, :, :, S:SP_], 0.0)
            nc.gpsimd.memset(ident_16[:, :], 0.0).then_inc(s_fill, 1)
            pool.wait_ge(s_fill, 3)
            nc.gpsimd.affine_select(out=ident_16[:, :], in_=ident_16[:, :], compare_op=ALU.not_equal, fill=1.0,
                                    base=0, pattern=[[-1, P]], channel_multiplier=1).then_inc(s_const, 1)
            nc.gpsimd.memset(minus_half[:, :], -0.5)
            nc.gpsimd.memset(ones[:, :], 1.0)
            nc.gpsimd.memset(attn[:, C:CC * P], 0.0)
            nc.gpsimd.memset(prob[:, :, TX:T], 0.0)
            for v in val:
                nc.gpsimd.memset(v[:, :, :, DH:DH + 1], 1.0)
                nc.gpsimd.memset(v[:, :, :, VW + DH:VW + DH + 1], 0.0)
            nc.gpsimd.memset(vip_diag[:, :, :], 0.0).then_inc(s_pool_set, 1)
            pool.wait_ge(s_ipsq, 1)
            pool.wait_ge(s_pool_set, 1)
            nc.gpsimd.tensor_tensor(ip_norm[:, 2:3], ip_norm[:, 1:2], minus_half[0:B * NIP, 0:1], ALU.pow).then_inc(s_pool_set, 1)

            def residual(a):
                pool.wait_ge(s_x, 16 * (a.n + 1))
                reached(pool, s_fin_ev, NF * (a.n - 1))
                nc.gpsimd.tensor_tensor(x_bias[a.odd][:, :], x_sb[:, 0:C], bias_sb[:, :], ALU.add).then_inc(s_xbias, 1)

            def batch_k_ip(a):
                reached(pool, s_val, H * (a.n - 1))
                nc.gpsimd.tensor_copy(kip_st[a.odd][:, :, :], kip_all[:, :, bass.ds(a.n * NIP, NIP)]).then_inc(s_kip, 1)

            pool.wait_ge(s_small, 32)
            pool.wait_ge(s_kip_st, 16 * 16)
            residual(Batch(0, 0, 0))
            batch_k_ip(Batch(0, 0, 0))

            def duals(b, h):
                g = H * b.n + h
                pool.wait_ge(s_prob_16, g + 1)
                reached(pool, s_quad, g - 1)
                nc.gpsimd.tensor_tensor(dual[:, h % 2, :], prob[:, h % 4, 0:TX], prob_16[:, h % 2, :], ALU.subtract).then_inc(s_dual, 1)

            def end(f, step):
                if step == VALS_STEP:
                    hs = half_sb[f.odd]
                    pool.wait_ge(s_half, 2 * f.n + 2)
                    reached(pool, s_text_out, f.n)
                    reached(pool, s_fin_arg, f.n)
                    for half in range(2):
                        o = hs[:, half, 0:OW].rearrange("s (h w) -> s h w", w=2 * VW)
                        last = nc.gpsimd.tensor_tensor(vals[:, half * HH:(half + 1) * HH, :], o[:, :, 0:VW], o[:, :, VW:2 * VW], ALU.add)
                    last.then_inc(s_vals, 1)
                if step in POW_STEPS:
                    h0 = POW_STEPS.index(step) * POW_HEADS
                    pool.wait_ge(s_n2, f.n + 1)
                    nc.gpsimd.tensor_tensor(nrm[:, 3, h0:h0 + POW_HEADS], nrm[:, 2, h0:h0 + POW_HEADS],
                                            minus_half[0:S, 0:POW_HEADS], ALU.pow).then_inc(s_rn, 1)
                if step == TEXT_OUT_STEP:
                    pool.wait_ge(s_vals, f.n + 1)
                    reached(pool, s_fin_ev, NF * f.n)
                    nc.gpsimd.tensor_tensor(text_out[:, :].rearrange("s (h d) -> s h d", d=DH), vals[:, :, 0:DH],
                                            rsum[:, :].unsqueeze(2).to_broadcast([S, H, DH]), ALU.mult).then_inc(s_text_out, 1)

            duals(Batch(0, 0, 0), 0)

            def body(b, prepare, finishing):
                for h in range(H):
                    if h + 1 < H:
                        duals(b, h + 1)
                    elif prepare:
                        duals(b.next(), 0)
                    if finishing:
                        end(b.last(), h)
                    if prepare and h == K_IP_STEP:
                        batch_k_ip(b.next())
                    if prepare and h == RESIDUAL_STEP:
                        residual(b.next())

            def tail(b):
                for step in range(TEXT_OUT_STEP + 1):
                    end(b.last(), step)

            all_batches(pool, body, tail)

        @block.tensor
        def _(pe):
            def split3(dst, parts_l, parts_r, chunks):
                n, total = 0, 3 * chunks
                for c in range(chunks):
                    for a, b_ in ((0, 0), (0, 1), (1, 0)):
                        last = nc.tensor.matmul(dst, parts_l(a, c), parts_r(b_, c), start=(n == 0), stop=(n == total - 1))
                        n += 1
                return last

            text = (text_hi, text_lo)
            w = (w_hi, w_lo)

            def prep(a, k, banks=(ps_prep,)):
                ps_prep = banks[k % len(banks)]
                done = max(k + 1 - len(banks), {PIECES_K[0]: PIECES_K[0], PIECE_Q: PIECE_X + 1, PIECE_GT: PIECE_GT}.get(k, 0))
                reached(pe, s_prep_lo, NA * a.n + done)
                reached(pe, s_prep_hi, NA * a.n + done)
                if k in PIECES_TEXT:
                    i = k - PIECES_TEXT[0]
                    if isinstance(a.n, int) and a.n == 0:
                        pe.wait_ge(s_ctx0[i], 16)
                    elif i == 0:
                        pe.wait_ge(s_ctx, 16 * a.n)
                    for e in range(EC):
                        last = nc.tensor.transpose(ps_prep[:, e * TC:(e + 1) * TC], ctx_sb[:, i, e * P:(e + 1) * P], ident[0:TC, 0:TC])
                elif k == PIECE_X:
                    pe.wait_ge(s_x, 16 * (a.n + 1))
                    for c in range(CC):
                        last = nc.tensor.transpose(ps_prep[:, c * S:(c + 1) * S], x_sb[:, c * P:(c + 1) * P], ident[0:S, 0:S])
                elif k in PIECES_K:
                    j = k - PIECES_K[0]
                    m = channels(j)
                    last = split3(ps_prep[0:m, 0:TX], lambda h_, e: w[h_][:, e, 0, j * P:j * P + m],
                                  lambda h_, e: text[h_][:, e, 0:TX], EC)
                elif k == PIECE_Q:
                    for j in range(CC):
                        for c in range(CC):
                            last = nc.tensor.matmul(ps_prep[:, j * S:(j + 1) * S], wq_sb[0:channels(c), c, j * P:(j + 1) * P],
                                                    x_T[0:channels(c), c, :], start=(c == 0), stop=(c == CC - 1))
                elif k in PIECES_G:
                    i = k - PIECES_G[0]
                    m, n0 = TROWS[i], i * TC
                    last = split3(ps_prep[:, 0:T - n0], lambda h_, e: text[h_][:, e, n0:n0 + P],
                                  lambda h_, e: text[h_][:, e, n0:T], EC)
                elif k == PIECE_GT:
                    g, blocks = gram_hi[a.odd], ps_prep[:, :].bitcast(F16)
                    for n, (i, j) in enumerate(((0, 1), (0, 2), (1, 2))):
                        last = nc.tensor.transpose(blocks[0:TROWS[j], n * P:n * P + TC], g[:, i, j * TC:j * TC + TROWS[j]],
                                                   ident_16[0:TC, 0:TC])
                else:
                    i = k - PIECES_V[0]
                    m, n0 = TROWS[i], i * TC
                    last = split3(ps_prep[:, 0:C], lambda h_, e: text[h_][:, e, n0:n0 + P],
                                  lambda h_, e: w[h_][:, e, 1, :], EC)
                last.then_inc(s_prep, 1)

            def scores(b, h):
                g = H * b.n + h
                if h == 0:
                    pe.wait_ge(s_kst[b.odd], 256 * (b.pair + 1))
                    pe.wait_ge(s_qst[b.odd], 256 * (b.pair + 1))
                reached(pe, s_prob, g - 1)
                nc.tensor.matmul(ps_score[h % 2][:, 0:TX], q_st[b.odd][:, h // 2, h % 2, :], k_st[b.odd][:, h // 2, :],
                                 start=True, stop=True).then_inc(s_score, 1)

            def transposes(b, h):
                g = H * b.n + h
                pe.wait_ge(s_prob, g + 1)
                reached(pe, s_pT_lo, g)
                for i in range(NT):
                    last = nc.tensor.transpose(ps_pT[0:TC, i * S:(i + 1) * S], prob[:, h % 4, i * TC:(i + 1) * TC],
                                               ident[0:S, 0:S])
                last.then_inc(s_pT, 1)

            def products(b, h):
                g = H * b.n + h
                if h == 0:
                    pe.wait_ge(s_prep_lo, NA * (b.n + 1))
                    pe.wait_ge(s_kip, b.n + 1)
                pe.wait_ge(s_pT_lo, g + 1)
                reached(pe, s_quad, g - 1)
                gh, gl, v = gram_hi[b.odd], gram_lo[b.odd], val[b.odd]
                hh = h % HH
                if hh == 0:
                    reached(pe, s_half, 2 * b.n + h // HH)
                o = hh * 2 * VW
                for i in range(NT):
                    r, first, last = TROWS[i], i == 0, i == NT - 1
                    hi, lo = pT_hi[0:r, h % 2, i, :], pT_lo[0:r, h % 2, i, :]
                    nc.tensor.matmul(ps_gram[h % 2][:, 0:TX], hi, gh[0:r, i, :], start=first, stop=False, skip_group_check=True)
                    gram = nc.tensor.matmul(ps_gram[h % 2][:, i * TC:TX], hi, gl[0:r, i, i * TC:TX], start=False, stop=last,
                                            skip_group_check=True)
                    nc.tensor.matmul(ps_val[:, o:o + 2 * VW], hi, v[0:r, i, h, :], start=first, stop=False, skip_group_check=True)
                    nc.tensor.matmul(ps_val[:, o:o + VW], lo, v[0:r, i, h, 0:VW], start=False, stop=last, skip_group_check=True)
                    if last:
                        gram.then_inc(s_gram, 1)
                nc.tensor.matmul(ps_val[:, OW + hh * NIP:OW + (hh + 1) * NIP], q_st[b.odd][:, h // 2, h % 2, :],
                                 kip_st[b.odd][:, h // 2, :], start=True, stop=True, skip_group_check=True).then_inc(s_val, 1)

            def finish(f, k):
                reached(pe, s_fin_ev, NF * f.n + k)
                if k == 0:
                    pe.wait_ge(s_fprob, f.n + 1)
                    last = nc.tensor.transpose(ps_fin[0:H * NIP, 0:S], fprob[:, :, :].rearrange("s h n -> s (h n)"), ident[0:S, 0:S])
                elif k == 1:
                    pe.wait_ge(s_vip_in, 16 * H)
                    last = nc.tensor.matmul(ps_fin[0:S, 0:C], fprob_T[:, :], vip_diag[:, f.n, :] if isinstance(f.n, int)
                                            else vip_diag[:, bass.ds(f.n, 1), :].rearrange("p a c -> p (a c)"), start=True, stop=True)
                elif k == 2:
                    for c in range(CC):
                        last = nc.tensor.transpose(ps_fin[:, c * S:(c + 1) * S], attn[:, c * P:(c + 1) * P], ident[0:S, 0:S])
                else:
                    pe.wait_ge(s_wo, 32)
                    for c in range(CC):
                        last = nc.tensor.matmul(ps_fin[0:S, 0:C], attn_T[0:channels(c), c, :], wo_sb[0:channels(c), c, :],
                                                start=(c == 0), stop=(c == CC - 1))
                last.then_inc(s_fin, 1)

            start = Batch(0, 0, 0)
            pe.wait_ge(s_const, 1)
            for k in (*PIECES_TEXT, PIECE_X):
                prep(start, k, SETUP_BANKS)
            pe.wait_ge(s_ip, 16 * B)
            for e in range(EC):
                last = nc.tensor.transpose(ps_val[:, e * 64:(e + 1) * 64], ip_rows[:, e * P:(e + 1) * P], ident[0:64, 0:64])
            last.then_inc(s_setup_pe, 1)
            pe.wait_ge(s_wsplit_lo, 1)
            for k in PIECES_K:
                prep(start, k, SETUP_BANKS)
            pe.wait_ge(s_wq, 32)
            prep(start, PIECE_Q, SETUP_BANKS)
            pe.wait_ge(s_setup_ev, 1)
            pe.wait_ge(s_w[2], 16)
            for j in range(CC):
                for e in range(EC):
                    last = nc.tensor.matmul(ps_fin[0:channels(j), j * 64:(j + 1) * 64], w_raw[:, e, 2, j * P:j * P + channels(j)],
                                            ip_T[:, e, :], start=(e == 0), stop=(e == EC - 1))
            last.then_inc(s_setup_pe, 1)
            pe.wait_ge(s_const, 3)
            for k in (*PIECES_G, PIECE_GT):
                prep(start, k, SETUP_BANKS)
            pe.wait_ge(s_w[3], 16)
            for e in range(EC):
                last = nc.tensor.matmul(ps_val[0:64, 0:C], ip_T[:, e, :], w_raw[:, e, 3, :], start=(e == 0), stop=(e == EC - 1))
            last.then_inc(s_setup_pe, 1)
            pe.wait_ge(s_ipdiag, 1)
            pe.wait_ge(s_setup_ev, 3)
            nc.tensor.matmul(ps_fin[0:S, 0:64], ones[:, :], ip_diag[:, :], start=True, stop=True).then_inc(s_setup_pe, 1)
            pe.wait_ge(s_wsplit_lo, 2)
            for k in PIECES_V:
                prep(start, k, SETUP_BANKS)
            scores(start, 0)
            scores(start, 1)
            transposes(start, 0)
            pe.wait_ge(s_prep_lo, NA)
            pe.wait_ge(s_setup_ev, 5)

            def body(b, prepare, finishing):
                for h in range(H):
                    if h + 2 < H:
                        scores(b, h + 2)
                    elif prepare:
                        scores(b.next(), h + 2 - H)
                    if h + 1 < H:
                        transposes(b, h + 1)
                    elif prepare:
                        transposes(b.next(), 0)
                    products(b, h)
                    if prepare and h in PREP_STEP:
                        prep(b.next(), PREP_STEP[h])
                    if finishing and h in FINISH_STEP:
                        finish(b.last(), FINISH_STEP[h])

            def tail(b):
                for k in range(NF):
                    finish(b.last(), k)

            all_batches(pe, body, tail)

        @block.scalar
        def _(act):
            def prep_hi(a, k, banks=(ps_prep,)):
                ps_prep = banks[k % len(banks)]
                act.wait_ge(s_prep, NA * a.n + k + 1)
                if k in PIECES_TEXT:
                    i = k - PIECES_TEXT[0]
                    last = nc.scalar.activation(text_hi[:, :, i * TC:(i + 1) * TC],
                                                ps_prep[:, 0:EC * TC].rearrange("p (e t) -> p e t", t=TC), ACT.Copy)
                elif k == PIECE_X:
                    last = nc.scalar.activation(x_T[:, 0:CC - 1, :].rearrange("p c s -> p (c s)"), ps_prep[:, 0:(CC - 1) * S], ACT.Copy)
                elif k in PIECES_K:
                    j = k - PIECES_K[0]
                    if j == 0:
                        reached(act, s_kst[1 - a.odd], 256 * (a.last().pair + 1))
                    m = channels(j)
                    last = nc.scalar.activation(k_hi[0:m, j, :], ps_prep[0:m, 0:TX], ACT.Copy, scale=1.0 / W_UP)
                elif k == PIECE_Q:
                    reached(act, s_qst[1 - a.odd], 256 * (a.last().pair + 1))
                    for e in range(2):
                        last = nc.scalar.activation(q_hi[:, :, e, 0:S], ps_prep[:, 0:CC * S].rearrange("p (c s) -> p c s", s=S),
                                                    ACT.Copy, scale=q_mask[:, e:e + 1])
                elif k in PIECES_G:
                    i = k - PIECES_G[0]
                    m, n0 = TROWS[i], i * TC
                    if i == 0:
                        reached(act, s_val, H * (a.n - 1))
                    nc.scalar.activation(gram_hi[a.odd][0:m, i, n0:TX], ps_prep[0:m, 0:TX - n0], ACT.Copy, scale=G_DOWN)
                    if i < NT - 1:
                        nc.scalar.activation(gram_2hi[0:m, i, n0 + m:TX], ps_prep[0:m, m:TX - n0], ACT.Copy, scale=2 * G_DOWN)
                    last = nc.scalar.activation(val[a.odd][0:m, i, :, DH + 1:VW],
                                                ps_prep[0:m, TX - n0:T - n0].unsqueeze(1).to_broadcast([m, H, NIP]), ACT.Copy, scale=G_DOWN)
                elif k == PIECE_GT:
                    last = nc.scalar.activation(gram_hi[a.odd][:, 1, 0:TC], ps_prep[0:TC, :].bitcast(F16)[:, 0:TC], ACT.Copy)
                else:
                    i = k - PIECES_V[0]
                    m = TROWS[i]
                    last = nc.scalar.activation(val[a.odd][0:m, i, :, 0:DH], ps_prep[0:m, 0:C].rearrange("p (h d) -> p h d", d=DH),
                                                ACT.Copy, scale=1.0 / W_UP)
                last.then_inc(s_prep_hi, 1)

            def exps(b, h):
                g = H * b.n + h
                act.wait_ge(s_low, g + 1)
                reached(act, s_dual, g - 3)
                nc.scalar.activation(prob[:, h % 4, 0:TX], ps_score[h % 2][0:S, 0:TX], ACT.Exp, bias=low[:, h % 4:h % 4 + 1],
                                     scale=-1.0).then_inc(s_prob, 1)

            def probs_hi(b, h):
                g = H * b.n + h
                act.wait_ge(s_pT, g + 1)
                reached(act, s_val, g - 1)
                nc.scalar.activation(pT_hi[:, h % 2, :, 0:S], ps_pT[0:TC, 0:NT * S].rearrange("p (c s) -> p c s", s=S), ACT.Copy).then_inc(s_pT_hi, 1)

            def halve(b, h):
                g = H * b.n + h
                act.wait_ge(s_prob, g + 1)
                reached(act, s_dual, g - 1)
                nc.scalar.activation(prob_16[:, h % 2, :], prob[:, h % 4, 0:TX], ACT.Copy, scale=0.5).then_inc(s_prob_16, 1)

            def half_out(b, half):
                act.wait_ge(s_val, H * b.n + (half + 1) * HH)
                if half == 0:
                    reached(act, s_text_out, b.n - 1)
                    reached(act, s_fin_arg, b.n - 1)
                nc.scalar.activation(half_sb[b.odd][:, half, :], ps_val[0:S, 0:HALF_W], ACT.Copy).then_inc(s_half, 1)

            def fin_exp(f):
                act.wait_ge(s_fin_arg, f.n + 1)
                reached(act, s_fprob, f.n)
                nc.scalar.activation(fexp[:, :, :], fused[:, :, :], ACT.Exp).then_inc(s_fin_exp, 1)

            def store(f):
                act.wait_ge(s_fin_ev, NF * (f.n + 1))
                act.dma_start(out[f.n, :, :], out_sb[:, :]).then_inc(s_store, 16)

            w_drams = (w_k, w_v, w_k_ip, w_v_ip)
            for i in (0, 2, 1, 3):
                act.dma_start(w_raw[:, :, i, :], w_drams[i].rearrange("(c p) n -> p c n", p=P)).then_inc(s_w[i], 16)
                if i == 0:
                    act.wait_ge(s_zero, 1)
                    load_rows(act, wq_sb, w_q, s_wq)
            start = Batch(0, 0, 0)

            def split_weight(i):
                act.wait_ge(s_w[i], 16)
                nc.scalar.activation(w_hi[:, :, i, :], w_raw[:, :, i, :], ACT.Copy, scale=W_UP).then_inc(s_wsplit_hi, 1)

            for k in (*PIECES_TEXT, PIECE_X):
                prep_hi(start, k, SETUP_BANKS)
            split_weight(0)
            act.wait_ge(s_qmask, 1)
            for k in (*PIECES_K, PIECE_Q):
                prep_hi(start, k, SETUP_BANKS)
            split_weight(1)
            for k in (*PIECES_G, PIECE_GT, *PIECES_V):
                prep_hi(start, k, SETUP_BANKS)
            exps(start, 0)
            probs_hi(start, 0)
            exps(start, 1)
            halve(start, 0)

            def body(b, prepare, finishing):
                for h in range(H):
                    if h + 1 < H:
                        probs_hi(b, h + 1)
                    elif prepare:
                        probs_hi(b.next(), 0)
                    if h + 2 < H:
                        exps(b, h + 2)
                    elif prepare:
                        exps(b.next(), h + 2 - H)
                    if h + 1 < H:
                        halve(b, h + 1)
                    elif prepare:
                        halve(b.next(), 0)
                    if h % HH == HH - 1:
                        half_out(b, h // HH)
                    if prepare and h in PREP_STEP:
                        prep_hi(b.next(), PREP_STEP[h])
                    if finishing and h == EXP_STEP:
                        fin_exp(b.last())
                    if finishing and h == H - 1:
                        store(b.last())

            def tail(b):
                fin_exp(b.last())
                store(b.last())
                act.wait_ge(s_store, 16 * B)

            all_batches(act, body, tail)

        @block.vector
        def _(dve):
            def low_part(out_, psum, scale, hi):
                return nc.vector.scalar_tensor_tensor(out=out_, in0=psum, scalar=scale, in1=hi, op0=ALU.mult, op1=ALU.subtract)

            def prep_lo(a, k, banks=(ps_prep,)):
                ps_prep = banks[k % len(banks)]
                dve.wait_ge(s_prep_hi, NA * a.n + k + 1)
                if k in PIECES_TEXT:
                    i = k - PIECES_TEXT[0]
                    last = nc.vector.tensor_tensor(text_lo[:, :, i * TC:(i + 1) * TC],
                                                   ps_prep[:, 0:EC * TC].rearrange("p (e t) -> p e t", t=TC),
                                                   text_hi[:, :, i * TC:(i + 1) * TC], ALU.subtract)
                elif k == PIECE_X:
                    last = nc.vector.tensor_copy(x_T[:, CC - 1, :], ps_prep[:, (CC - 1) * S:CC * S])
                elif k in PIECES_K:
                    j = k - PIECES_K[0]
                    m = channels(j)
                    if j == 0:
                        reached(dve, s_kst[1 - a.odd], 256 * (a.last().pair + 1))
                    last = low_part(k_lo[0:m, j, :], ps_prep[0:m, 0:TX], 1.0 / W_UP, k_hi[0:m, j, :])
                elif k == PIECE_Q:
                    reached(dve, s_qst[1 - a.odd], 256 * (a.last().pair + 1))
                    for e in range(2):
                        last = low_part(q_lo[:, :, e, 0:S], ps_prep[:, 0:CC * S].rearrange("p (c s) -> p c s", s=S),
                                        q_mask[:, e:e + 1], q_hi[:, :, e, 0:S])
                elif k in PIECES_G:
                    i = k - PIECES_G[0]
                    m, n0 = TROWS[i], i * TC
                    if i == 0:
                        reached(dve, s_val, H * (a.n - 1))
                    g, gl, v = gram_hi[a.odd], gram_lo[a.odd], val[a.odd]
                    low_part(gl[0:m, i, n0:n0 + m], ps_prep[0:m, 0:m], G_DOWN, g[0:m, i, n0:n0 + m])
                    if i < NT - 1:
                        low_part(gl[0:m, i, n0 + m:TX], ps_prep[0:m, m:TX - n0], 2 * G_DOWN, gram_2hi[0:m, i, n0 + m:TX])
                    last = low_part(v[0:m, i, :, VW + DH + 1:2 * VW],
                                    ps_prep[0:m, TX - n0:T - n0].unsqueeze(1).to_broadcast([m, H, NIP]), G_DOWN, v[0:m, i, :, DH + 1:VW])
                elif k == PIECE_GT:
                    r = TROWS[2]
                    last = nc.vector.tensor_copy(gram_hi[a.odd][0:r, 2, 0:2 * TC].rearrange("p (i t) -> p i t", t=TC),
                                                 ps_prep[0:r, :].bitcast(F16)[:, P:3 * P].rearrange("p (i t) -> p i t", t=P)[:, :, 0:TC])
                else:
                    i = k - PIECES_V[0]
                    m = TROWS[i]
                    last = low_part(val[a.odd][0:m, i, :, VW:VW + DH], ps_prep[0:m, 0:C].rearrange("p (h d) -> p h d", d=DH),
                                    1.0 / W_UP, val[a.odd][0:m, i, :, 0:DH])
                last.then_inc(s_prep_lo, 1)

            def minimum(b, h):
                g = H * b.n + h
                dve.wait_ge(s_score, g + 1)
                reached(dve, s_prob, g - 3)
                nc.vector.tensor_reduce(low[:, h % 4:h % 4 + 1], ps_score[h % 2][0:S, 0:TX], AX.X, ALU.min).then_inc(s_low, 1)

            def probs_lo(b, h):
                g = H * b.n + h
                dve.wait_ge(s_pT_hi, g + 1)
                nc.vector.tensor_tensor(pT_lo[:, h % 2, :, 0:S], ps_pT[0:TC, 0:NT * S].rearrange("p (c s) -> p c s", s=S),
                                        pT_hi[:, h % 2, :, 0:S], ALU.subtract).then_inc(s_pT_lo, 1)

            def quadratic(b, h):
                g = H * b.n + h
                dve.wait_ge(s_gram, g + 1)
                dve.wait_ge(s_dual, g + 1)
                nc.vector.tensor_tensor_reduce(out=quad_junk[:, h % 2, :], in0=ps_gram[h % 2][0:S, 0:TX], in1=dual[:, h % 2, :], scale=1.0,
                                               scalar=0.0, op0=ALU.mult, op1=ALU.add,
                                               accum_out=quad[b.odd][:, h:h + 1]).then_inc(s_quad, 1)

            def chain(f, k, ins):
                ins.then_inc(s_chain, 1)
                dve.wait_ge(s_chain, FINAL_CHAIN * f.n + SETUP_CHAIN + k + 1)

            def soft(f, part):
                def over_ip(v):
                    return v.unsqueeze(2).to_broadcast([S, H, NIP])

                if part == 0:
                    dve.wait_ge(s_vals, f.n + 1)
                    dve.wait_ge(s_quad, H * (f.n + 1))
                    reached(dve, s_text_out, f.n)
                    chain(f, 0, nc.vector.reciprocal(rsum[:, :], vals[:, :, DH]))
                    chain(f, 1, nc.vector.tensor_tensor(nrm[:, 0, :], quad[f.odd][:, :], rsum[:, :], ALU.mult))
                    chain(f, 2, nc.vector.tensor_tensor(nrm[:, 1, :], nrm[:, 0, :], rsum[:, :], ALU.mult))
                    nc.vector.tensor_scalar(nrm[:, 2, :], nrm[:, 1, :], 2.0 / G_DOWN, EPS * EPS, ALU.mult, ALU.max).then_inc(s_n2, 1)
                elif part == 1:
                    dve.wait_ge(s_rn, len(POW_STEPS) * (f.n + 1))
                    reached(dve, s_fin_exp, f.n)
                    chain(f, 3, nc.vector.tensor_tensor(nrm[:, 0, :], nrm[:, 3, :], rsum[:, :], ALU.mult))
                    chain(f, 4, nc.vector.tensor_tensor(fused[:, :, :], vals[:, :, DH + 1:VW], over_ip(nrm[:, 0, :]), ALU.mult))
                    inv = ip_inv[:, bass.ds(f.n * NIP, NIP)].unsqueeze(1).to_broadcast([S, H, NIP])
                    chain(f, 5, nc.vector.tensor_tensor(fused[:, :, :], fused[:, :, :], inv, ALU.mult))
                    ip_score = half_sb[f.odd][:, :, OW:HALF_W].rearrange("s a (h n) -> s a h n", n=NIP)
                    halves = fused[:, :, :].rearrange("s (a h) n -> s a h n", a=2)
                    chain(f, 6, nc.vector.tensor_tensor(halves, halves, ip_score, ALU.subtract))
                    chain(f, 7, nc.vector.tensor_reduce(fmax[:, 0, :], fused[:, :, :], AX.X, ALU.max))
                    nc.vector.tensor_tensor(fused[:, :, :], fused[:, :, :], over_ip(fmax[:, 0, :]), ALU.subtract).then_inc(s_fin_arg, 1)
                else:
                    dve.wait_ge(s_fin_exp, f.n + 1)
                    reached(dve, s_fin, NF * f.n)
                    chain(f, 8, nc.vector.tensor_reduce(fmax[:, 1, :], fexp[:, :, :], AX.X, ALU.add))
                    chain(f, 9, nc.vector.reciprocal(fmax[:, 2, :], fmax[:, 1, :]))
                    chain(f, 10, nc.vector.tensor_scalar(fmax[:, 1, :], fmax[:, 2, :], mask_sb[:, 0:1], None, ALU.mult))
                    nc.vector.tensor_tensor(fprob[:, :, :], fexp[:, :, :], over_ip(fmax[:, 1, :]), ALU.mult).then_inc(s_fprob, 1)

            def finish(f, k):
                dve.wait_ge(s_fin, NF * f.n + k + 1)
                if k == 0:
                    last = nc.vector.tensor_copy(fprob_T[:, :], ps_fin[0:H * NIP, 0:S])
                elif k == 1:
                    dve.wait_ge(s_text_out, f.n + 1)
                    last = nc.vector.tensor_tensor(attn[:, 0:C], ps_fin[0:S, 0:C], text_out[:, :], ALU.add)
                elif k == 2:
                    last = nc.vector.tensor_copy(attn_T[:, :, :].rearrange("p c s -> p (c s)"), ps_fin[:, 0:CC * S])
                else:
                    reached(dve, s_store, 16 * f.n)
                    last = nc.vector.tensor_tensor(out_sb[:, :], ps_fin[0:S, 0:C], x_bias[f.odd][:, :], ALU.add)
                last.then_inc(s_fin_ev, 1)

            start = Batch(0, 0, 0)
            dve.wait_ge(s_const, 2)
            nc.vector.tensor_reduce(q_mask[:, :], head_rows[:, :, :], AX.X, ALU.add).then_inc(s_chain, 1)
            dve.wait_ge(s_chain, 1)
            nc.vector.tensor_scalar(q_mask[:, :], q_mask[:, :], -Q_SCALE, None, ALU.mult).then_inc(s_qmask, 1)
            for k in (*PIECES_TEXT, PIECE_X):
                prep_lo(start, k, SETUP_BANKS)
            dve.wait_ge(s_setup_pe, 1)
            nc.vector.tensor_copy(ip_T[:, :, :].rearrange("p e t -> p (e t)"), ps_val[:, 0:EC * 64]).then_inc(s_setup_ev, 1)
            dve.wait_ge(s_wsplit_hi, 1)
            low_part(w_lo[:, :, 0, :], w_raw[:, :, 0, :], W_UP, w_hi[:, :, 0, :]).then_inc(s_wsplit_lo, 1)
            dve.wait_ge(s_ip, 16 * B)
            nc.vector.tensor_tensor_reduce(out=ip_sq[:, :], in0=ip_rows[:, :], in1=ip_rows[:, :], scale=1.0, scalar=0.0,
                                           op0=ALU.mult, op1=ALU.add, accum_out=ip_norm[:, 0:1]).then_inc(s_chain, 1)
            dve.wait_ge(s_chain, 2)
            nc.vector.tensor_scalar(ip_norm[:, 1:2], ip_norm[:, 0:1], EPS * EPS, None, ALU.max).then_inc(s_ipsq, 1)
            for k in (*PIECES_K, PIECE_Q):
                prep_lo(start, k, SETUP_BANKS)
            dve.wait_ge(s_setup_pe, 2)
            for m, c0, c1 in ((P, 0, CC - 1), (CR, CC - 1, CC)):
                last = nc.vector.tensor_copy(kip_hi[0:m, c0:c1, :].rearrange("p c t -> p (c t)"), ps_fin[0:m, c0 * 64:c1 * 64])
            last.then_inc(s_setup_ev, 1)
            dve.wait_ge(s_setup_ev, 2)
            for m, c0, c1 in ((P, 0, CC - 1), (CR, CC - 1, CC)):
                last = nc.vector.tensor_tensor(kip_lo[0:m, c0:c1, :].rearrange("p c t -> p (c t)"), ps_fin[0:m, c0 * 64:c1 * 64],
                                               kip_hi[0:m, c0:c1, :].rearrange("p c t -> p (c t)"), ALU.subtract)
            last.then_inc(s_setup_ev, 1)
            for k in (*PIECES_G, PIECE_GT):
                prep_lo(start, k, SETUP_BANKS)
            dve.wait_ge(s_pool_set, 2)
            nc.vector.tensor_scalar(ip_norm[:, 3:4], ip_norm[:, 2:3], SEM_SCALE / G_DOWN, None, ALU.mult).then_inc(s_chain, 1)
            dve.wait_ge(s_chain, 3)
            nc.vector.tensor_scalar(ip_diag[:, :], ident[0:64, 0:64], ip_norm[:, 3:4], None, ALU.mult).then_inc(s_ipdiag, 1)
            dve.wait_ge(s_setup_pe, 3)
            nc.vector.tensor_copy(vip_rows[:, :], ps_val[0:64, 0:C]).then_inc(s_setup_ev, 1)
            dve.wait_ge(s_wsplit_hi, 2)
            low_part(w_lo[:, :, 1, :], w_raw[:, :, 1, :], W_UP, w_hi[:, :, 1, :]).then_inc(s_wsplit_lo, 1)
            dve.wait_ge(s_setup_pe, 4)
            nc.vector.tensor_copy(ip_inv[:, :], ps_fin[0:S, 0:64]).then_inc(s_setup_ev, 1)
            for k in PIECES_V:
                prep_lo(start, k, SETUP_BANKS)
            dve.wait_ge(s_small, 32)
            minimum(start, 0)
            minimum(start, 1)
            probs_lo(start, 0)

            def body(b, prepare, finishing):
                for h in range(H):
                    if h + 2 < H:
                        minimum(b, h + 2)
                    elif prepare:
                        minimum(b.next(), h + 2 - H)
                    if prepare and h - 1 in PREP_STEP:
                        prep_lo(b.next(), PREP_STEP[h - 1])
                    if finishing and h - 1 in FINISH_STEP:
                        finish(b.last(), FINISH_STEP[h - 1])
                    if h + 1 < H:
                        probs_lo(b, h + 1)
                    elif prepare:
                        probs_lo(b.next(), 0)
                    quadratic(b, h)
                    if finishing and h in (NORM_STEP, ARG_STEP, PROB_STEP):
                        soft(b.last(), (NORM_STEP, ARG_STEP, PROB_STEP).index(h))

            def tail(b):
                for part in range(3):
                    soft(b.last(), part)
                for k in range(NF):
                    finish(b.last(), k)

            all_batches(dve, body, tail)


_INS = ['x', 'ctx_2048', 'fside_S_0', 'L0_xattn_W_q', 'L0_xattn_W_k', 'L0_xattn_W_v', 'L0_xattn_W_k_ip', 'L0_xattn_W_v_ip',
        'L0_xattn_W_out', 'L0_xattn_b_out']


def kernel(**inputs):
    import numpy as np
    import concourse.bacc as bacc
    from concourse.bass_utils import run_bass_kernel_spmd

    nc = bacc.Bacc("TRN2", target_bir_lowering=False, num_devices=1)
    arrays, args = {}, []
    for name in _INS:
        a = np.ascontiguousarray(inputs[name])
        arrays[f"in_{name}"] = a
        args.append(nc.dram_tensor(f"in_{name}", a.shape, mybir.dt.from_np(a.dtype), kind="ExternalInput").ap())
    args.append(nc.dram_tensor("out_0", (B, S, C), F32, kind="ExternalOutput").ap())
    build(nc, *args)
    r = run_bass_kernel_spmd(nc, [arrays], core_ids=[0])
    return r.results[0]["out_0"]
```

```python
import concourse.bass as bass
from concourse import mybir
from concourse.alu_op_type import AluOpType as ALU
from contextlib import ExitStack

F32 = mybir.dt.float32
F16 = mybir.dt.float16
ACT = mybir.ActivationFunctionType
AX = mybir.AxisListType

B, S, C = 16, 112, 320
T, E = 375, 512
NIP = 4
TX = T - NIP
H = 20
DH = C // H
P = 128
EC = E // P
CC = (C + P - 1) // P
CR = C - (CC - 1) * P
TC = T // 3
NT = 3
TROWS = [min(TC, TX - i * TC) for i in range(NT)]
NG = C // 32
HH = H // 2
VW = DH + 1 + NIP
OW = HH * 2 * VW
HALF_W = OW + HH * NIP
EPS = 1e-12
SEM_SCALE = 0.5
W_UP = 64.0
G_DOWN = 1.0 / 64.0
Q_SCALE = DH ** -0.5

NM = 10
PIECE_Q, PIECES_K, PIECES_V, PIECES_G = 0, (1, 2, 3), (4, 5, 9), (6, 7, 8)
PIECE_TURN_G = PIECES_G[-1]
TURNED_G = 160
G_DIAG = 384
NL = 4
MAKE_STEP = {2 * k: k for k in range(NM)}
NX = 4
PIECES_TEXT, PIECE_X = (0, 1, 2), 3
TURN_STEP = {1: 0, 3: 1, 5: 2, 11: 3}
NF = 4
FINISH_STEP = {13: 0, 15: 1, 17: 2, 18: 3}
VALS_STEP, POW_STEPS, EXP_STEP = 0, (3, 4, 5, 6), 10
SOFT_AT = {(2, 0): 0, (2, 1): 1, (2, 2): 2, (3, 0): 3,
           (8, 0): 4, (8, 1): 5, (8, 2): 6, (9, 0): 7, (9, 1): 8, (9, 2): 9,
           (11, 0): 10, (11, 1): 11, (11, 2): 12, (12, 0): 13}
SOFT_LATER = 1
SOFT = len(SOFT_AT)
SOFT_NORMS, SOFT_ARGS = 4, 10
TEXT_OUT_STEP = 8
K_IP_STEP, RESIDUAL_STEP = 1, 19
POW_HEADS = H // len(POW_STEPS)
AHEAD_VALS_STEP, AHEAD_NORM_STEPS, AHEAD_POW_STEPS = 14, (15, 16, 17, 18), (18, 19)
S_PAD = P
T_PAD = NT * P


def channels(j):
    return P if j < CC - 1 else CR


class Batch:

    def __init__(self, n, odd, pair):
        self.n, self.odd, self.pair = n, odd, pair

    def next(self):
        return Batch(self.n + 1, 1 - self.odd, self.pair + self.odd)

    def last(self):
        return Batch(self.n - 1, 1 - self.odd, self.pair - (1 - self.odd))


def build(nc, x, ctx, mask, w_q, w_k, w_v, w_k_ip, w_v_ip, w_out, b_out, out):
    scratch = nc.dram_tensor("v_ip_scratch", (B * NIP, C), F32, kind="Internal").ap()
    stack = ExitStack()
    with stack:
        def sb(name, shape, dt=F32):
            return stack.enter_context(nc.sbuf_tensor(name, shape, dt))

        def ps(name, shape):
            return stack.enter_context(nc.psum_tensor(name, shape, F32))

        def sem(name):
            return stack.enter_context(nc.semaphore(name))

        ident = sb("ident", [P, P])
        ident_16 = sb("ident_16", [P, P], F16)
        ones = sb("ones", [64, S])
        head_rows = sb("head_rows", [P, 2, 4])
        q_mask = sb("q_mask", [P, 2])
        mask_sb = sb("mask_sb", [S, 1])
        bias_sb = sb("bias_sb", [S, C])
        wq_sb = sb("wq_sb", [P, CC, CC * P])
        wo_sb = sb("wo_sb", [P, CC, C])
        wq_hi = sb("wq_hi", [P, CC, CC * P], F16)
        wq_lo = sb("wq_lo", [P, CC, CC * P], F16)
        wo_hi = sb("wo_hi", [P, CC, C], F16)
        wo_lo = sb("wo_lo", [P, CC, C], F16)
        w_raw = sb("w_raw", [P, EC, 4, C])
        w_hi = sb("w_hi", [P, EC, 2, C], F16)
        w_lo = sb("w_lo", [P, EC, 2, C], F16)
        wk_last = sb("wk_last", [P, EC, 2, CR], F16)
        ip_rows = sb("ip_rows", [B * NIP, E])
        ip_sq = sb("ip_sq", [B * NIP, E])
        ip_norm = sb("ip_norm", [B * NIP, 4])
        minus_half = sb("minus_half", [P, H])
        ip_diag = sb("ip_diag", [B * NIP, B * NIP])
        ip_inv = sb("ip_inv", [S, NIP, B])
        ip_T = sb("ip_T", [P, EC, B * NIP])
        kip_hi = sb("kip_hi", [P, CC, NIP, B], F16)
        kip_lo = sb("kip_lo", [P, CC, NIP, B], F16)
        vip_rows = sb("vip_rows", [B * NIP, C])
        vip_diag = sb("vip_diag", [H * NIP, B, C])
        ctx_sb = sb("ctx_sb", [TC, NT, E])
        x_sb = [sb(f"x_sb{i}", [S, CC * P]) for i in range(2)]
        x_bias = [sb(f"x_bias{i}", [S, C]) for i in range(2)]
        text_hi = [sb(f"text_hi{i}", [P, EC, T_PAD], F16) for i in range(2)]
        text_lo = [sb(f"text_lo{i}", [P, EC, T_PAD], F16) for i in range(2)]
        x_hi = sb("x_hi", [P, CC, S], F16)
        x_lo = sb("x_lo", [P, CC, S], F16)
        k_hi = sb("k_hi", [P, CC, T], F16)
        k_lo = sb("k_lo", [P, CC, T], F16)
        q_hi = sb("q_hi", [P, CC, 2, S_PAD], F16)
        q_lo = sb("q_lo", [P, CC, 2, S_PAD], F16)
        k_st = [sb(f"k_st{i}", [P, NG, T], F16) for i in range(2)]
        q_st = [sb(f"q_st{i}", [P, NG, 2, S_PAD], F16) for i in range(2)]
        gram_hi = [sb(f"gram_hi{i}", [TC, NT, TX], F16) for i in range(2)]
        gram_lo = [sb(f"gram_lo{i}", [TC, NT, TX], F16) for i in range(2)]
        gram_2hi = sb("gram_2hi", [TC, 2, TX], F16)
        val = [sb(f"val{i}", [TC, NT, H, 2 * VW], F16) for i in range(2)]
        low = sb("low", [S, 4])
        prob = sb("prob", [S, 4, T])
        pT_hi = sb("pT_hi", [TC, 2, NT, S_PAD], F16)
        pT_lo = sb("pT_lo", [TC, 2, NT, S_PAD], F16)
        prob_16 = sb("prob_16", [S, 2, TX], F16)
        dual = sb("dual", [S, 2, TX])
        quad_junk = sb("quad_junk", [S, 2, TX])
        quad = [sb(f"quad{i}", [S, H]) for i in range(2)]
        half_sb = [sb(f"half_sb{i}", [S, 2, HALF_W]) for i in range(2)]
        vals = sb("vals", [S, H, VW])
        rsum = sb("rsum", [S, H])
        nrm = sb("nrm", [S, 4, H])
        fused = sb("fused", [S, H, NIP])
        fmax = sb("fmax", [S, 3, H])
        fexp = sb("fexp", [S, H, NIP])
        fprob = sb("fprob", [S, H, NIP])
        fprob_T = sb("fprob_T", [H * NIP, S])
        text_out = sb("text_out", [S, C])
        attn = sb("attn", [S, CC * P])
        attn_hi = sb("attn_hi", [P, CC, S], F16)
        attn_lo = sb("attn_lo", [P, CC, S], F16)
        out_sb = sb("out_sb", [S, C])

        ps_score = [ps(f"ps_score{i}", [P, 512]) for i in range(2)]
        ps_pT = ps("ps_pT", [P, 512])
        ps_gram = [ps(f"ps_gram{i}", [P, 512]) for i in range(2)]
        ps_val = ps("ps_val", [P, 512])
        ps_prep = ps("ps_prep", [P, 512])
        ps_light = ps("ps_light", [P, 512])

        s_w = [sem(f"s_w{i}") for i in range(4)]
        s_wq, s_wo, s_ip = sem("s_wq"), sem("s_wo"), sem("s_ip")
        s_small = sem("s_small")
        s_ctx, s_x = sem("s_ctx"), [sem(f"s_x{i}") for i in range(2)]
        s_ctx0 = [sem(f"s_ctx0_{i}") for i in range(NT)]
        s_vip_out, s_vip_in = sem("s_vip_out"), sem("s_vip_in")
        s_kst = [sem(f"s_kst{i}") for i in range(2)]
        s_qst = [sem(f"s_qst{i}") for i in range(2)]
        s_store = sem("s_store")
        s_zero, s_const, s_qmask, s_wsplit_hi, s_wsplit_lo = (sem(n) for n in ("s_zero", "s_const", "s_qmask", "s_wsplit_hi", "s_wsplit_lo"))
        s_wk_last = sem("s_wk_last")
        s_pool_set, s_fill, s_ipsq, s_ipdiag = sem("s_pool_set"), sem("s_fill"), sem("s_ipsq"), sem("s_ipdiag")
        s_setup_pe, s_setup_ev = sem("s_setup_pe"), sem("s_setup_ev")
        s_prep, s_prep_hi, s_prep_lo, s_part_lo = sem("s_prep"), sem("s_prep_hi"), sem("s_prep_lo"), sem("s_part_lo")
        s_turn, s_turn_hi, s_turn_lo = sem("s_turn"), sem("s_turn_hi"), sem("s_turn_lo")
        s_xbias, s_kip = sem("s_xbias"), sem("s_kip")
        s_score, s_low, s_prob = sem("s_score"), sem("s_low"), sem("s_prob")
        s_pT, s_pT_hi, s_pT_lo = sem("s_pT"), sem("s_pT_hi"), sem("s_pT_lo")
        s_prob_16, s_dual = sem("s_prob_16"), sem("s_dual")
        s_gram, s_val, s_quad, s_half = sem("s_gram"), sem("s_val"), sem("s_quad"), sem("s_half")
        s_ahead = sem("s_ahead")
        s_vals, s_chain, s_soft, s_rn = sem("s_vals"), sem("s_chain"), sem("s_soft"), sem("s_rn")
        s_fin_exp, s_attn_hi = sem("s_fin_exp"), sem("s_attn_hi")
        s_text_out, s_fin, s_fin_ev = sem("s_text_out"), sem("s_fin"), sem("s_fin_ev")

        SETUP_BANKS = (ps_prep, ps_gram[0], ps_gram[1])
        TURN_BANKS = (*ps_score, ps_pT, ps_light)

        block = stack.enter_context(nc.Block())

        def reached(eng, s, value):
            if not (isinstance(value, int) and value <= 0):
                eng.wait_ge(s, value)

        def all_batches(eng, body, tail):
            pairs = B // 2
            body(Batch(0, 0, 0), True, True, False)
            body(Batch(1, 1, 0), True, True, True)
            with eng.Fori(1, pairs - 1) as i:
                body(Batch(2 * i, 0, i), True, True, True)
                body(Batch(2 * i + 1, 1, i), True, True, True)
            body(Batch(B - 2, 0, pairs - 1), True, False, True)
            body(Batch(B - 1, 1, pairs - 1), False, False, True)
            tail(Batch(B, 0, pairs))

        def load_rows(eng, dst, src, s):
            eng.dma_start(dst[:, 0:CC - 1, 0:C], src[0:(CC - 1) * P, :].rearrange("(c p) n -> p c n", p=P)).then_inc(s, 16)
            eng.dma_start(dst[0:CR, CC - 1, 0:C], src[(CC - 1) * P:C, :]).then_inc(s, 16)

        def load_context_weight(eng, i):
            eng.dma_start(w_raw[:, :, i, :], (w_k, w_v, w_k_ip, w_v_ip)[i].rearrange("(c p) n -> p c n", p=P)).then_inc(s_w[i], 16)

        def restack(dst, srcs, terms):
            return [(dst[32 * term:32 * term + 32, q::4], srcs[term][32 * q:32 * q + 32, 0:len(range(q, NG, 4))])
                    for q in range(4) for term in terms]

        def q_restack(odd, terms):
            return restack(q_st[odd], (q_hi, q_hi, q_lo, q_lo), terms)

        def k_restack(odd, terms):
            return restack(k_st[odd], (k_hi, k_lo, k_hi, k_lo), terms)

        @block.sync
        def _(sp):
            def load_ctx(a):
                sp.wait_ge(s_turn, NX * (a.n - 1) + PIECES_TEXT[-1] + 1)
                sp.dma_start(ctx_sb[:, :, :], ctx[a.n, :, :].rearrange("(c p) e -> p c e", p=TC)).then_inc(s_ctx, 16)

            def load_x(a):
                reached(sp, s_turn, NX * (a.n - 2) + PIECE_X + 1)
                reached(sp, s_xbias, a.n - 1)
                sp.dma_start(x_sb[a.odd][:, 0:C], x[a.n, :, :]).then_inc(s_x[a.odd], 16)

            def stack_kq(a, q_terms=range(4), k_terms=range(4)):
                reached(sp, s_score, H * (a.n - 1))
                sp.wait_ge(s_prep_lo, NM * a.n + PIECE_Q + 1)
                for dst, src in q_restack(a.odd, q_terms):
                    sp.dma_start(dst, src).then_inc(s_qst[a.odd], 16)
                sp.wait_ge(s_prep_lo, NM * a.n + PIECES_K[-1] + 1)
                sp.wait_ge(s_kip, a.n + 1)
                for dst, src in k_restack(a.odd, k_terms):
                    sp.dma_start(dst, src).then_inc(s_kst[a.odd], 16)

            def spread_v_ip():
                sp.wait_ge(s_setup_ev, 4)
                sp.dma_start(scratch[:, :], vip_rows[:, :]).then_inc(s_vip_out, 16)
                sp.wait_ge(s_vip_out, 16)
                sp.wait_ge(s_pool_set, 1)
                vip_view = scratch.rearrange("(n b) c -> n b c", n=NIP)
                for h in range(H):
                    sp.dma_start(vip_diag[h * NIP:(h + 1) * NIP, :, h * DH:(h + 1) * DH],
                                 vip_view[:, :, h * DH:(h + 1) * DH]).then_inc(s_vip_in, 16)

            for c in range(NT):
                sp.dma_start(ctx_sb[:, c, :], ctx[0, c * TC:(c + 1) * TC, :]).then_inc(s_ctx0[c], 16)
            sp.wait_ge(s_zero, 1)
            load_x(Batch(0, 0, 0))
            for n in range(NIP):
                sp.dma_start(ip_rows[n * B:(n + 1) * B, :], ctx[:, TX + n, :]).then_inc(s_ip, 16)
            load_context_weight(sp, 2)
            load_context_weight(sp, 1)
            load_x(Batch(1, 1, 0))
            load_ctx(Batch(1, 1, 0))
            load_context_weight(sp, 3)
            sp.dma_start(bias_sb[:, :], b_out.partition_broadcast(S)).then_inc(s_small, 16)
            sp.dma_start(mask_sb[:, :], mask.rearrange("(s a) -> s a", a=1)).then_inc(s_small, 16)
            sp.wait_ge(s_const, 3)
            stack_kq(Batch(0, 0, 0), (0, 1), (0, 1, 2))
            load_rows(sp, wo_sb, w_out, s_wo)

            def body(b, prepare, turning, finishing):
                if turning:
                    load_ctx(b.next().next())
                    load_x(b.next().next())
                if isinstance(b.n, int) and b.n == 0:
                    spread_v_ip()
                if prepare:
                    stack_kq(b.next())

            all_batches(sp, body, lambda b: None)

        @block.gpsimd
        def _(pool):
            for x_ in x_sb:
                nc.gpsimd.memset(x_[:, C:CC * P], 0.0)
            nc.gpsimd.memset(wq_sb[:, 0:CC - 1, C:CC * P], 0.0)
            for w_ in (wq_sb, wo_sb):
                last = nc.gpsimd.memset(w_[:, CC - 1, :], 0.0)
            last.then_inc(s_zero, 1)
            nc.gpsimd.memset(ident[:, :], 0.0)
            nc.gpsimd.memset(head_rows[:, :, :], 1.0).then_inc(s_fill, 1)
            pool.wait_ge(s_fill, 1)
            nc.gpsimd.affine_select(out=ident[:, :], in_=ident[:, :], compare_op=ALU.not_equal, fill=1.0,
                                    base=0, pattern=[[-1, P]], channel_multiplier=1).then_inc(s_const, 1)
            nc.gpsimd.affine_select(out=head_rows[:, :, :], in_=head_rows[:, :, :], compare_op=ALU.is_ge, fill=0.0,
                                    base=0, pattern=[[-DH, 2], [-2 * DH, 4]], channel_multiplier=1).then_inc(s_fill, 1)
            pool.wait_ge(s_fill, 2)
            nc.gpsimd.affine_select(out=head_rows[:, :, :], in_=head_rows[:, :, :], compare_op=ALU.is_ge, fill=0.0,
                                    base=DH - 1, pattern=[[DH, 2], [2 * DH, 4]], channel_multiplier=-1).then_inc(s_const, 1)
            for t_ in (*text_hi, *text_lo):
                nc.gpsimd.memset(t_[:, :, T:T_PAD], 0.0)
            for t_ in (q_hi, q_lo, pT_hi, pT_lo):
                nc.gpsimd.memset(t_[:, :, :, S:S_PAD], 0.0)
            for t_ in (kip_hi, kip_lo):
                nc.gpsimd.memset(t_[:, CC - 1, :, :], 0.0)
            nc.gpsimd.memset(ident_16[:, :], 0.0).then_inc(s_fill, 1)
            pool.wait_ge(s_fill, 3)
            nc.gpsimd.affine_select(out=ident_16[:, :], in_=ident_16[:, :], compare_op=ALU.not_equal, fill=1.0,
                                    base=0, pattern=[[-1, P]], channel_multiplier=1).then_inc(s_const, 1)
            nc.gpsimd.memset(minus_half[:, :], -0.5)
            nc.gpsimd.memset(ones[:, :], 1.0)
            nc.gpsimd.memset(attn[:, C:CC * P], 0.0)
            nc.gpsimd.memset(prob[:, :, TX:T], 0.0)
            for v in val:
                nc.gpsimd.memset(v[:, :, :, DH:DH + 1], 1.0)
                nc.gpsimd.memset(v[:, :, :, VW + DH:VW + DH + 1], 0.0)
            nc.gpsimd.memset(vip_diag[:, :, :], 0.0).then_inc(s_pool_set, 1)
            def residual(a):
                pool.wait_ge(s_x[a.odd], 16 * (a.pair + 1))
                reached(pool, s_fin_ev, NF * (a.n - 1))
                nc.gpsimd.tensor_tensor(x_bias[a.odd][:, :], x_sb[a.odd][:, 0:C], bias_sb[:, :], ALU.add).then_inc(s_xbias, 1)

            def batch_k_ip(a):
                reached(pool, s_kst[1 - a.odd], 256 * (a.last().pair + 1))
                for k_, ip in ((k_hi, kip_hi), (k_lo, kip_lo)):
                    last = nc.gpsimd.tensor_copy(k_[:, :, TX:T], ip[:, :, :, bass.ds(a.n, 1)].rearrange("p c n a -> p c (n a)"))
                last.then_inc(s_kip, 1)

            pool.wait_ge(s_setup_ev, 3)
            batch_k_ip(Batch(0, 0, 0))
            pool.wait_ge(s_ipsq, 1)
            pool.wait_ge(s_pool_set, 1)
            nc.gpsimd.tensor_tensor(ip_norm[:, 2:3], ip_norm[:, 1:2], minus_half[0:B * NIP, 0:1], ALU.pow).then_inc(s_pool_set, 1)
            pool.wait_ge(s_small, 32)
            residual(Batch(0, 0, 0))

            def duals(b, h):
                g = H * b.n + h
                pool.wait_ge(s_prob_16, g + 1)
                reached(pool, s_quad, g - 1)
                nc.gpsimd.tensor_tensor(dual[:, h % 2, :], prob[:, h % 4, 0:TX], prob_16[:, h % 2, :], ALU.subtract).then_inc(s_dual, 1)

            def sum_values(f, half):
                pool.wait_ge(s_half, 2 * f.n + half + 1)
                o = half_sb[f.odd][:, half, 0:OW].rearrange("s (h w) -> s h w", w=2 * VW)
                return nc.gpsimd.tensor_tensor(vals[:, half * HH:(half + 1) * HH, :], o[:, :, 0:VW], o[:, :, VW:2 * VW], ALU.add)

            def inverse_roots(part):
                h0 = part * POW_HEADS
                nc.gpsimd.tensor_tensor(nrm[:, 3, h0:h0 + POW_HEADS], nrm[:, 2, h0:h0 + POW_HEADS],
                                        minus_half[0:S, 0:POW_HEADS], ALU.pow).then_inc(s_rn, 1)

            def end(f, step, ahead=False):
                if step == VALS_STEP:
                    reached(pool, s_text_out, f.n)
                    reached(pool, s_soft, SOFT * (f.n - 1) + SOFT_ARGS)
                    if not ahead:
                        sum_values(f, 0)
                    sum_values(f, 1).then_inc(s_vals, 1)
                if step in POW_STEPS and not (ahead and POW_STEPS.index(step) * POW_HEADS < HH):
                    pool.wait_ge(s_soft, SOFT * f.n + SOFT_NORMS)
                    inverse_roots(POW_STEPS.index(step))
                if step == TEXT_OUT_STEP:
                    pool.wait_ge(s_vals, f.n + 1)
                    reached(pool, s_fin_ev, NF * f.n)
                    nc.gpsimd.tensor_tensor(text_out[:, :].rearrange("s (h d) -> s h d", d=DH), vals[:, :, 0:DH],
                                            rsum[:, :].unsqueeze(2).to_broadcast([S, H, DH]), ALU.mult).then_inc(s_text_out, 1)

            duals(Batch(0, 0, 0), 0)

            def body(b, prepare, turning, finishing):
                for h in range(H):
                    if h + 1 < H:
                        duals(b, h + 1)
                    elif prepare:
                        duals(b.next(), 0)
                    if finishing:
                        end(b.last(), h)
                    if not prepare and h == AHEAD_VALS_STEP:
                        pool.wait_ge(s_text_out, b.n)
                        pool.wait_ge(s_soft, SOFT * (b.n - 1) + SOFT_ARGS)
                        sum_values(b, 0).then_inc(s_ahead, 1)
                    if not prepare and h in AHEAD_POW_STEPS:
                        pool.wait_ge(s_ahead, 1 + SOFT_NORMS)
                        inverse_roots(AHEAD_POW_STEPS.index(h))
                    if prepare and h == K_IP_STEP:
                        batch_k_ip(b.next())
                    if prepare and h == RESIDUAL_STEP:
                        residual(b.next())

            def tail(b):
                for step in range(TEXT_OUT_STEP + 1):
                    end(b.last(), step, ahead=True)

            all_batches(pool, body, tail)

        @block.tensor
        def _(pe):
            def split3(dst, parts_l, parts_r, chunks):
                n, total = 0, 3 * chunks
                for c in range(chunks):
                    for a, b_ in ((0, 0), (0, 1), (1, 0)):
                        last = nc.tensor.matmul(dst, parts_l(a, c), parts_r(b_, c), start=(n == 0), stop=(n == total - 1))
                        n += 1
                return last

            w = (w_hi, w_lo)

            def light_bank_free(turned, finished):
                reached(pe, s_turn_lo, turned)
                reached(pe, s_turn_hi, turned)
                reached(pe, s_fin_ev, finished)

            def turn(a, k, banks=(ps_light,)):
                bank = banks[k % len(banks)]
                if k in PIECES_TEXT:
                    i = k - PIECES_TEXT[0]
                    if isinstance(a.n, int) and a.n == 0:
                        pe.wait_ge(s_ctx0[i], 16)
                    elif i == 0:
                        pe.wait_ge(s_ctx, 16 * a.n)
                    for e in range(EC):
                        last = nc.tensor.transpose(bank[:, e * TC:(e + 1) * TC], ctx_sb[:, i, e * P:(e + 1) * P], ident[0:TC, 0:TC])
                else:
                    pe.wait_ge(s_x[a.odd], 16 * (a.pair + 1))
                    for c in range(CC):
                        last = nc.tensor.transpose(bank[:, c * S:(c + 1) * S], x_sb[a.odd][:, c * P:(c + 1) * P], ident[0:S, 0:S])
                last.then_inc(s_turn, 1)

            def make(a, k, banks=(ps_prep,)):
                bank = banks[k % len(banks)]
                text = (text_hi[a.odd], text_lo[a.odd])
                reached(pe, s_prep_lo, NM * a.n + k + 1 - len(banks))
                if k == PIECE_Q:
                    pe.wait_ge(s_turn_lo, NX * (a.n + 1))
                    pe.wait_ge(s_turn_hi, NX * (a.n + 1))
                if k == PIECES_K[0]:
                    pe.wait_ge(s_turn_lo, NX * a.n + PIECES_TEXT[-1] + 1)
                if k == PIECE_TURN_G:
                    pe.wait_ge(s_prep_hi, NM * a.n + PIECES_G[1] + 1)
                if k in PIECES_K:
                    j = k - PIECES_K[0]
                    m = channels(j)
                    if j < CC - 1:
                        last = split3(bank[:, 0:TX], lambda h_, e: w[h_][:, e, 0, j * P:(j + 1) * P],
                                      lambda h_, e: text[h_][:, e, 0:TX], EC)
                    else:
                        if isinstance(a.n, int) and a.n == 0:
                            pe.wait_ge(s_wk_last, 2)
                        for e in range(EC):
                            nc.tensor.matmul(bank[:, 0:TX], wk_last[:, e, :, :].rearrange("p a c -> p (a c)"), text[0][:, e, 0:TX],
                                             start=(e == 0), stop=(e == EC - 1), skip_group_check=True)
                            last = nc.tensor.matmul(bank[0:m, 0:TX], wk_last[:, e, 0, :], text[1][:, e, 0:TX],
                                                    start=False, stop=(e == EC - 1), skip_group_check=True)
                elif k == PIECE_Q:
                    for j in range(CC):
                        last = split3(bank[:, j * S:(j + 1) * S], lambda h_, c: (wq_hi, wq_lo)[h_][0:channels(c), c, j * P:(j + 1) * P],
                                      lambda h_, c: (x_hi, x_lo)[h_][0:channels(c), c, :], CC)
                elif k in PIECES_G:
                    i = k - PIECES_G[0]
                    m, n0 = TROWS[i], i * TC
                    hi, lo = text
                    if k == PIECE_TURN_G:
                        g, blocks = gram_hi[a.odd], bank[:, TURNED_G:G_DIAG].bitcast(F16)
                        for n, (r0, c0) in enumerate(((0, 1), (0, 2), (1, 2))):
                            nc.tensor.transpose(blocks[0:TROWS[c0], n * P:n * P + TC], g[:, r0, c0 * TC:c0 * TC + TROWS[c0]], ident_16[0:TC, 0:TC])
                    for e in range(EC):
                        nc.tensor.matmul(bank[:, G_DIAG:G_DIAG + m], hi[:, e, n0:n0 + P], lo[:, e, n0:n0 + m],
                                         start=(e == 0), stop=(e == EC - 1))
                    for e in range(EC):
                        for part, l, r_, c in ((0, hi, hi, 0), (1, hi, lo, m), (2, lo, hi, m)):
                            last = nc.tensor.matmul(bank[:, c:T - n0], l[:, e, n0:n0 + P], r_[:, e, n0 + c:T],
                                                    start=(e == 0 and part == 0), stop=(e == EC - 1 and part == 2), skip_group_check=True)
                else:
                    i = PIECES_V.index(k)
                    m, n0 = TROWS[i], i * TC
                    last = split3(bank[:, 0:C], lambda h_, e: text[h_][:, e, n0:n0 + P],
                                  lambda h_, e: w[h_][:, e, 1, :], EC)
                last.then_inc(s_prep, 1)

            def scores(b, h):
                g = H * b.n + h
                if h == 0:
                    pe.wait_ge(s_kst[b.odd], 256 * (b.pair + 1))
                    pe.wait_ge(s_qst[b.odd], 256 * (b.pair + 1))
                reached(pe, s_prob, g - 1)
                nc.tensor.matmul(ps_score[h % 2][:, 0:TX], q_st[b.odd][:, h // 2, h % 2, :], k_st[b.odd][:, h // 2, 0:TX],
                                 start=True, stop=True).then_inc(s_score, 1)

            def transposes(b, h):
                g = H * b.n + h
                pe.wait_ge(s_prob, g + 1)
                reached(pe, s_pT_lo, g)
                for i in range(NT):
                    last = nc.tensor.transpose(ps_pT[0:TC, i * S:(i + 1) * S], prob[:, h % 4, i * TC:(i + 1) * TC],
                                               ident[0:S, 0:S])
                last.then_inc(s_pT, 1)

            def products(b, h):
                g = H * b.n + h
                if h == 0:
                    pe.wait_ge(s_prep_lo, NM * (b.n + 1))
                pe.wait_ge(s_pT_lo, g + 1)
                reached(pe, s_quad, g - 1)
                gh, gl, v = gram_hi[b.odd], gram_lo[b.odd], val[b.odd]
                hh = h % HH
                o = hh * 2 * VW

                def gram_part(i):
                    hi = pT_hi[0:TROWS[i], h % 2, i, :]
                    nc.tensor.matmul(ps_gram[h % 2][:, 0:TX], hi, gh[0:TROWS[i], i, :], start=(i == 0), stop=False, skip_group_check=True)
                    last = nc.tensor.matmul(ps_gram[h % 2][:, i * TC:TX], hi, gl[0:TROWS[i], i, i * TC:TX], start=False,
                                            stop=(i == NT - 1), skip_group_check=True)
                    if i == NT - 1:
                        last.then_inc(s_gram, 1)

                def val_part(i):
                    r = TROWS[i]
                    nc.tensor.matmul(ps_val[:, o:o + 2 * VW], pT_hi[0:r, h % 2, i, :], v[0:r, i, h, :], start=(i == 0), stop=False,
                                     skip_group_check=True)
                    nc.tensor.matmul(ps_val[:, o:o + VW], pT_lo[0:r, h % 2, i, :], v[0:r, i, h, 0:VW], start=False,
                                     stop=(i == NT - 1), skip_group_check=True)

                if hh == 0:
                    for i in range(NT):
                        gram_part(i)
                    reached(pe, s_half, 2 * b.n + h // HH)
                    for i in range(NT):
                        val_part(i)
                else:
                    for i in range(NT):
                        gram_part(i)
                        val_part(i)
                nc.tensor.matmul(ps_val[:, OW + hh * NIP:OW + (hh + 1) * NIP], q_st[b.odd][:, h // 2, h % 2, :],
                                 k_st[b.odd][:, h // 2, TX:T], start=True, stop=True, skip_group_check=True).then_inc(s_val, 1)

            def finish(f, k):
                if k == 0:
                    pe.wait_ge(s_soft, SOFT * (f.n + 1))
                    last = nc.tensor.transpose(ps_light[0:H * NIP, 0:S], fprob[:, :, :].rearrange("s h n -> s (h n)"), ident[0:S, 0:S])
                elif k == 1:
                    pe.wait_ge(s_vip_in, 16 * H)
                    last = nc.tensor.matmul(ps_light[0:S, 0:C], fprob_T[:, :], vip_diag[:, f.n, :] if isinstance(f.n, int)
                                            else vip_diag[:, bass.ds(f.n, 1), :].rearrange("p a c -> p (a c)"), start=True, stop=True)
                elif k == 2:
                    for c in range(CC):
                        last = nc.tensor.transpose(ps_light[:, c * S:(c + 1) * S], attn[:, c * P:(c + 1) * P], ident[0:S, 0:S])
                else:
                    pe.wait_ge(s_wsplit_lo, 4)
                    last = split3(ps_light[0:S, 0:C], lambda h_, c: (attn_hi, attn_lo)[h_][0:channels(c), c, :],
                                  lambda h_, c: (wo_hi, wo_lo)[h_][0:channels(c), c, :], CC)
                last.then_inc(s_fin, 1)

            start, second = Batch(0, 0, 0), Batch(1, 1, 0)
            pe.wait_ge(s_const, 1)
            for k in range(NX):
                turn(start, k, TURN_BANKS)
            pe.wait_ge(s_ip, 16 * NIP)
            for e in range(EC):
                last = nc.tensor.transpose(ps_val[:, e * 64:(e + 1) * 64], ip_rows[:, e * P:(e + 1) * P], ident[0:64, 0:64])
            last.then_inc(s_setup_pe, 1)
            pe.wait_ge(s_wsplit_lo, 1)
            make(start, PIECE_Q, SETUP_BANKS)
            pe.wait_ge(s_wsplit_lo, 2)
            for k in PIECES_K:
                make(start, k, SETUP_BANKS)
            pe.wait_ge(s_setup_ev, 1)
            pe.wait_ge(s_w[2], 16)
            light_bank_free(NX, 0)
            for j in range(CC):
                for e in range(EC):
                    last = nc.tensor.matmul(ps_light[0:channels(j), j * 64:(j + 1) * 64], w_raw[:, e, 2, j * P:j * P + channels(j)],
                                            ip_T[:, e, :], start=(e == 0), stop=(e == EC - 1))
            last.then_inc(s_setup_pe, 1)
            pe.wait_ge(s_setup_ev, 3)
            for k in range(NX):
                turn(second, k, TURN_BANKS)
            pe.wait_ge(s_const, 3)
            pe.wait_ge(s_wsplit_lo, 3)
            for k in range(PIECES_V[0], PIECES_G[1]):
                make(start, k, SETUP_BANKS)
            pe.wait_ge(s_w[3], 16)
            for e in range(EC):
                last = nc.tensor.matmul(ps_val[0:64, 0:C], ip_T[:, e, :], w_raw[:, e, 3, :], start=(e == 0), stop=(e == EC - 1))
            last.then_inc(s_setup_pe, 1)
            for k in PIECES_G[1:]:
                make(start, k, SETUP_BANKS)
            pe.wait_ge(s_ipdiag, 1)
            light_bank_free(2 * NX, 0)
            nc.tensor.matmul(ps_light[0:S, 0:64], ones[:, :], ip_diag[:, :], start=True, stop=True).then_inc(s_setup_pe, 1)
            scores(start, 0)
            scores(start, 1)
            make(start, NM - 1, SETUP_BANKS)
            transposes(start, 0)
            scores(start, 2)
            pe.wait_ge(s_prep_lo, NM)
            pe.wait_ge(s_setup_ev, 5)

            def body(b, prepare, turning, finishing):
                turned, finished = (NX * (b.n + 2) if turning else NX * B), (NF * (b.n - 1) if finishing else 0)
                for h in range(H):
                    if h + 3 < H:
                        scores(b, h + 3)
                    elif prepare:
                        scores(b.next(), h + 3 - H)
                    if h + 1 < H:
                        transposes(b, h + 1)
                    elif prepare:
                        transposes(b.next(), 0)
                    products(b, h)
                    if prepare and h in MAKE_STEP:
                        make(b.next(), MAKE_STEP[h])
                    if turning and h in TURN_STEP:
                        light_bank_free(turned, finished)
                        turn(b.next().next(), TURN_STEP[h])
                        turned = turned + 1
                    if finishing and h in FINISH_STEP:
                        light_bank_free(turned, finished)
                        finish(b.last(), FINISH_STEP[h])
                        finished = finished + 1

            def tail(b):
                for k in range(NF):
                    light_bank_free(NX * B, NF * (B - 1) + k)
                    finish(b.last(), k)

            all_batches(pe, body, tail)

        @block.scalar
        def _(act):
            def turn_hi(a, k, banks=(ps_light,)):
                bank = banks[k % len(banks)]
                act.wait_ge(s_turn, NX * a.n + k + 1)
                if k in PIECES_TEXT:
                    i = k - PIECES_TEXT[0]
                    last = nc.scalar.activation(text_hi[a.odd][:, :, i * TC:(i + 1) * TC],
                                                bank[:, 0:EC * TC].rearrange("p (e t) -> p e t", t=TC), ACT.Copy)
                else:
                    last = nc.scalar.activation(x_hi[:, :, :].rearrange("p c s -> p (c s)"), bank[:, 0:CC * S], ACT.Copy)
                last.then_inc(s_turn_hi, 1)

            def make_hi(a, k, banks=(ps_prep,)):
                bank = banks[k % len(banks)]
                act.wait_ge(s_prep, NM * a.n + k + 1)
                if k in PIECES_K:
                    j = k - PIECES_K[0]
                    if j == 0:
                        reached(act, s_kst[1 - a.odd], 256 * (a.last().pair + 1))
                    m = channels(j)
                    last = nc.scalar.activation(k_hi[0:m, j, 0:TX], bank[0:m, 0:TX], ACT.Copy, scale=1.0 / W_UP)
                elif k == PIECE_Q:
                    reached(act, s_qst[1 - a.odd], 256 * (a.last().pair + 1))
                    for e in range(2):
                        last = nc.scalar.activation(q_hi[:, :, e, 0:S], bank[:, 0:CC * S].rearrange("p (c s) -> p c s", s=S),
                                                    ACT.Copy, scale=q_mask[:, e:e + 1])
                elif k in PIECES_G:
                    i = k - PIECES_G[0]
                    m, n0 = TROWS[i], i * TC
                    if k == PIECE_TURN_G:
                        nc.scalar.activation(gram_hi[a.odd][:, 1, 0:TC], bank[0:TC, TURNED_G:G_DIAG].bitcast(F16)[:, 0:TC], ACT.Copy)
                    nc.scalar.activation(gram_hi[a.odd][0:m, i, n0:TX], bank[0:m, 0:TX - n0], ACT.Copy, scale=G_DOWN)
                    if i < NT - 1:
                        nc.scalar.activation(gram_2hi[0:m, i, n0 + m:TX], bank[0:m, m:TX - n0], ACT.Copy, scale=2 * G_DOWN)
                    last = nc.scalar.activation(val[a.odd][0:m, i, :, DH + 1:VW],
                                                bank[0:m, TX - n0:T - n0].unsqueeze(1).to_broadcast([m, H, NIP]), ACT.Copy, scale=G_DOWN)
                else:
                    i = PIECES_V.index(k)
                    m = TROWS[i]
                    if i == 0:
                        reached(act, s_val, H * (a.n - 1))
                    last = nc.scalar.activation(val[a.odd][0:m, i, :, 0:DH], bank[0:m, 0:C].rearrange("p (h d) -> p h d", d=DH),
                                                ACT.Copy, scale=1.0 / W_UP)
                last.then_inc(s_prep_hi, 1)

            def exps(b, h):
                g = H * b.n + h
                act.wait_ge(s_low, g + 1)
                reached(act, s_dual, g - 3)
                nc.scalar.activation(prob[:, h % 4, 0:TX], ps_score[h % 2][0:S, 0:TX], ACT.Exp, bias=low[:, h % 4:h % 4 + 1],
                                     scale=-1.0).then_inc(s_prob, 1)

            def probs_hi(b, h):
                g = H * b.n + h
                act.wait_ge(s_pT, g + 1)
                reached(act, s_val, g - 1)
                nc.scalar.activation(pT_hi[:, h % 2, :, 0:S], ps_pT[0:TC, 0:NT * S].rearrange("p (c s) -> p c s", s=S), ACT.Copy).then_inc(s_pT_hi, 1)

            def halve(b, h):
                g = H * b.n + h
                act.wait_ge(s_prob, g + 1)
                reached(act, s_dual, g - 1)
                nc.scalar.activation(prob_16[:, h % 2, :], prob[:, h % 4, 0:TX], ACT.Copy, scale=0.5).then_inc(s_prob_16, 1)

            def half_out(b, half):
                act.wait_ge(s_val, H * b.n + (half + 1) * HH)
                if half == 0:
                    reached(act, s_text_out, b.n - 1)
                    reached(act, s_soft, SOFT * (b.n - 2) + SOFT_ARGS)
                nc.scalar.activation(half_sb[b.odd][:, half, :], ps_val[0:S, 0:HALF_W], ACT.Copy).then_inc(s_half, 1)

            def fin_exp(f):
                act.wait_ge(s_soft, SOFT * f.n + SOFT_ARGS)
                reached(act, s_soft, SOFT * f.n)
                nc.scalar.activation(fexp[:, :, :], fused[:, :, :], ACT.Exp).then_inc(s_fin_exp, 1)

            def attn_out(f):
                act.wait_ge(s_fin, NF * f.n + 3)
                nc.scalar.activation(attn_hi[:, :, :].rearrange("p c s -> p (c s)"), ps_light[:, 0:CC * S], ACT.Copy).then_inc(s_attn_hi, 1)

            def store(f):
                act.wait_ge(s_fin_ev, NF * (f.n + 1))
                act.dma_start(out[f.n, :, :], out_sb[:, :]).then_inc(s_store, 16)

            act.wait_ge(s_zero, 1)
            load_rows(act, wq_sb, w_q, s_wq)
            load_context_weight(act, 0)
            start = Batch(0, 0, 0)

            def split_weight(hi, raw, s, loads):
                act.wait_ge(s, 16 * loads)
                nc.scalar.activation(hi, raw, ACT.Copy, scale=W_UP).then_inc(s_wsplit_hi, 1)

            for k in range(NX):
                turn_hi(start, k, TURN_BANKS)
            split_weight(wq_hi[:, :, :], wq_sb[:, :, :], s_wq, 2)
            split_weight(w_hi[:, :, 0, :], w_raw[:, :, 0, :], s_w[0], 1)
            nc.scalar.activation(wk_last[:, :, 0, :], w_raw[:, :, 0, C - CR:C], ACT.Copy, scale=W_UP).then_inc(s_wk_last, 1)
            act.wait_ge(s_qmask, 1)
            for k in (PIECE_Q, *PIECES_K):
                make_hi(start, k, SETUP_BANKS)
            split_weight(w_hi[:, :, 1, :], w_raw[:, :, 1, :], s_w[1], 1)
            for k in range(NX):
                turn_hi(Batch(1, 1, 0), k, TURN_BANKS)
            for k in range(PIECES_V[0], NM - 1):
                make_hi(start, k, SETUP_BANKS)
            exps(start, 0)
            exps(start, 1)
            make_hi(start, NM - 1, SETUP_BANKS)
            probs_hi(start, 0)
            halve(start, 0)
            exps(start, 2)
            split_weight(wo_hi[:, :, :], wo_sb[:, :, :], s_wo, 2)

            def body(b, prepare, turning, finishing):
                for h in range(H):
                    if h + 1 < H:
                        probs_hi(b, h + 1)
                    elif prepare:
                        probs_hi(b.next(), 0)
                    if prepare and h - 1 in MAKE_STEP:
                        make_hi(b.next(), MAKE_STEP[h - 1])
                    if turning and h - 1 in TURN_STEP:
                        turn_hi(b.next().next(), TURN_STEP[h - 1])
                    if finishing and FINISH_STEP.get(h - 1) == 2:
                        attn_out(b.last())
                    if h + 3 < H:
                        exps(b, h + 3)
                    elif prepare:
                        exps(b.next(), h + 3 - H)
                    if h % HH == HH - 1:
                        half_out(b, h // HH)
                    if h + 1 < H:
                        halve(b, h + 1)
                    elif prepare:
                        halve(b.next(), 0)
                    if finishing and h == EXP_STEP + (0 if prepare else SOFT_LATER):
                        fin_exp(b.last())
                    if finishing and h == H - 1:
                        store(b.last())

            def tail(b):
                fin_exp(b.last())
                attn_out(b.last())
                store(b.last())
                act.wait_ge(s_store, 16 * B)

            all_batches(act, body, tail)

        @block.vector
        def _(dve):
            def low_part(out_, psum, scale, hi):
                return nc.vector.scalar_tensor_tensor(out=out_, in0=psum, scalar=scale, in1=hi, op0=ALU.mult, op1=ALU.subtract)

            def add_part(io, psum, scale):
                return nc.vector.scalar_tensor_tensor(out=io, in0=psum, scalar=scale, in1=io, op0=ALU.mult, op1=ALU.add)

            def turn_lo(a, k, banks=(ps_light,)):
                bank = banks[k % len(banks)]
                dve.wait_ge(s_turn_hi, NX * a.n + k + 1)
                if k in PIECES_TEXT:
                    i = k - PIECES_TEXT[0]
                    hi, lo = (t[a.odd][:, :, i * TC:(i + 1) * TC] for t in (text_hi, text_lo))
                    last = nc.vector.tensor_tensor(lo, bank[:, 0:EC * TC].rearrange("p (e t) -> p e t", t=TC), hi, ALU.subtract)
                else:
                    hi, lo = (t[:, :, :].rearrange("p c s -> p (c s)") for t in (x_hi, x_lo))
                    last = nc.vector.tensor_tensor(lo, bank[:, 0:CC * S], hi, ALU.subtract)
                last.then_inc(s_turn_lo, 1)

            def make_lo(a, k, banks=(ps_prep,)):
                bank = banks[k % len(banks)]
                dve.wait_ge(s_prep_hi, NM * a.n + k + 1)
                if k in PIECES_K:
                    j = k - PIECES_K[0]
                    m = channels(j)
                    if j == 0:
                        reached(dve, s_kst[1 - a.odd], 256 * (a.last().pair + 1))
                    last = low_part(k_lo[0:m, j, 0:TX], bank[0:m, 0:TX], 1.0 / W_UP, k_hi[0:m, j, 0:TX])
                    if k == PIECES_K[-1]:
                        last.then_inc(s_part_lo, 1)
                        dve.wait_ge(s_part_lo, NL * a.n + 1)
                        last = add_part(k_lo[0:m, j, 0:TX], bank[m:2 * m, 0:TX], 1.0 / W_UP)
                elif k == PIECE_Q:
                    reached(dve, s_qst[1 - a.odd], 256 * (a.last().pair + 1))
                    for e in range(2):
                        last = low_part(q_lo[:, :, e, 0:S], bank[:, 0:CC * S].rearrange("p (c s) -> p c s", s=S),
                                        q_mask[:, e:e + 1], q_hi[:, :, e, 0:S])
                elif k in PIECES_G:
                    i = k - PIECES_G[0]
                    m, n0 = TROWS[i], i * TC
                    g, gl, v = gram_hi[a.odd], gram_lo[a.odd], val[a.odd]
                    low_part(gl[0:m, i, n0:n0 + m], bank[0:m, 0:m], G_DOWN, g[0:m, i, n0:n0 + m]).then_inc(s_part_lo, 1)
                    if i < NT - 1:
                        low_part(gl[0:m, i, n0 + m:TX], bank[0:m, m:TX - n0], 2 * G_DOWN, gram_2hi[0:m, i, n0 + m:TX])
                    low_part(v[0:m, i, :, VW + DH + 1:2 * VW],
                             bank[0:m, TX - n0:T - n0].unsqueeze(1).to_broadcast([m, H, NIP]), G_DOWN, v[0:m, i, :, DH + 1:VW])
                    if k == PIECE_TURN_G:
                        nc.vector.tensor_copy(g[0:m, 2, 0:2 * TC].rearrange("p (i t) -> p i t", t=TC),
                                              bank[0:m, TURNED_G:G_DIAG].bitcast(F16)[:, P:3 * P].rearrange("p (i t) -> p i t", t=P)[:, :, 0:TC])
                    dve.wait_ge(s_part_lo, NL * a.n + 2 + i)
                    last = add_part(gl[0:m, i, n0:n0 + m], bank[0:m, G_DIAG:G_DIAG + m], 2 * G_DOWN)
                else:
                    i = PIECES_V.index(k)
                    m = TROWS[i]
                    if i == 0:
                        reached(dve, s_val, H * (a.n - 1))
                    last = low_part(val[a.odd][0:m, i, :, VW:VW + DH], bank[0:m, 0:C].rearrange("p (h d) -> p h d", d=DH),
                                    1.0 / W_UP, val[a.odd][0:m, i, :, 0:DH])
                last.then_inc(s_prep_lo, 1)

            def minimum(b, h):
                g = H * b.n + h
                dve.wait_ge(s_score, g + 1)
                reached(dve, s_prob, g - 3)
                nc.vector.tensor_reduce(low[:, h % 4:h % 4 + 1], ps_score[h % 2][0:S, 0:TX], AX.X, ALU.min).then_inc(s_low, 1)

            def probs_lo(b, h):
                g = H * b.n + h
                dve.wait_ge(s_pT_hi, g + 1)
                nc.vector.tensor_tensor(pT_lo[:, h % 2, :, 0:S], ps_pT[0:TC, 0:NT * S].rearrange("p (c s) -> p c s", s=S),
                                        pT_hi[:, h % 2, :, 0:S], ALU.subtract).then_inc(s_pT_lo, 1)

            def quadratic(b, h):
                g = H * b.n + h
                dve.wait_ge(s_gram, g + 1)
                dve.wait_ge(s_dual, g + 1)
                nc.vector.tensor_tensor_reduce(out=quad_junk[:, h % 2, :], in0=ps_gram[h % 2][0:S, 0:TX], in1=dual[:, h % 2, :], scale=1.0,
                                               scalar=0.0, op0=ALU.mult, op1=ALU.add,
                                               accum_out=quad[b.odd][:, h:h + 1]).then_inc(s_quad, 1)

            def norms(f, k, h0, h1):
                r, n = rsum[:, h0:h1], nrm[:, :, h0:h1]
                if k == 0:
                    return nc.vector.reciprocal(r, vals[:, h0:h1, DH])
                if k == 1:
                    return nc.vector.tensor_tensor(n[:, 0, :], quad[f.odd][:, h0:h1], r, ALU.mult)
                if k == 2:
                    return nc.vector.tensor_tensor(n[:, 1, :], n[:, 0, :], r, ALU.mult)
                return nc.vector.tensor_scalar(n[:, 2, :], n[:, 1, :], 2.0 / G_DOWN, EPS * EPS, ALU.mult, ALU.max)

            def norms_ahead(f, k):
                dve.wait_ge(s_ahead, k + 1)
                if k == 0:
                    dve.wait_ge(s_quad, H * f.n + HH)
                    dve.wait_ge(s_text_out, f.n)
                norms(f, k, 0, HH).then_inc(s_ahead, 1)

            def soft(f, k, ahead=False):
                def over_ip(v):
                    return v.unsqueeze(2).to_broadcast([S, H, NIP])

                v, reduce, pair = nc.vector, nc.vector.tensor_reduce, nc.vector.tensor_tensor
                if k:
                    reached(dve, s_soft, SOFT * f.n + k)
                if k < SOFT_NORMS:
                    if k == 0:
                        dve.wait_ge(s_vals, f.n + 1)
                        dve.wait_ge(s_quad, H * (f.n + 1))
                        reached(dve, s_text_out, f.n)
                    last = norms(f, k, HH if ahead else 0, H)
                elif k == 4:
                    dve.wait_ge(s_rn, len(POW_STEPS) * (f.n + 1))
                    reached(dve, s_fin_exp, f.n)
                    last = pair(nrm[:, 0, :], nrm[:, 3, :], rsum[:, :], ALU.mult)
                elif k == 5:
                    last = pair(fused[:, :, :], vals[:, :, DH + 1:VW], over_ip(nrm[:, 0, :]), ALU.mult)
                elif k == 6:
                    inv = ip_inv[:, :, bass.ds(f.n, 1)].rearrange("s n b -> s b n").to_broadcast([S, H, NIP])
                    last = pair(fused[:, :, :], fused[:, :, :], inv, ALU.mult)
                elif k == 7:
                    ip_score = half_sb[f.odd][:, :, OW:HALF_W].rearrange("s a (h n) -> s a h n", n=NIP)
                    halves = fused[:, :, :].rearrange("s (a h) n -> s a h n", a=2)
                    last = pair(halves, halves, ip_score, ALU.subtract)
                elif k == 8:
                    last = reduce(fmax[:, 0, :], fused[:, :, :], AX.X, ALU.max)
                elif k == 9:
                    last = pair(fused[:, :, :], fused[:, :, :], over_ip(fmax[:, 0, :]), ALU.subtract)
                elif k == 10:
                    dve.wait_ge(s_fin_exp, f.n + 1)
                    last = reduce(fmax[:, 1, :], fexp[:, :, :], AX.X, ALU.add)
                elif k == 11:
                    last = v.reciprocal(fmax[:, 2, :], fmax[:, 1, :])
                elif k == 12:
                    last = v.tensor_scalar(fmax[:, 1, :], fmax[:, 2, :], mask_sb[:, 0:1], None, ALU.mult)
                else:
                    reached(dve, s_fin, NF * f.n)
                    last = pair(fprob[:, :, :], fexp[:, :, :], over_ip(fmax[:, 1, :]), ALU.mult)
                last.then_inc(s_soft, 1)

            def finish(f, k):
                dve.wait_ge(s_fin, NF * f.n + k + 1)
                if k == 0:
                    last = nc.vector.tensor_copy(fprob_T[:, :], ps_light[0:H * NIP, 0:S])
                elif k == 1:
                    dve.wait_ge(s_text_out, f.n + 1)
                    last = nc.vector.tensor_tensor(attn[:, 0:C], ps_light[0:S, 0:C], text_out[:, :], ALU.add)
                elif k == 2:
                    dve.wait_ge(s_attn_hi, f.n + 1)
                    hi, lo = (t[:, :, :].rearrange("p c s -> p (c s)") for t in (attn_hi, attn_lo))
                    last = nc.vector.tensor_tensor(lo, ps_light[:, 0:CC * S], hi, ALU.subtract)
                else:
                    reached(dve, s_store, 16 * f.n)
                    last = nc.vector.scalar_tensor_tensor(out=out_sb[:, :], in0=ps_light[0:S, 0:C], scalar=1.0 / W_UP, in1=x_bias[f.odd][:, :],
                                                          op0=ALU.mult, op1=ALU.add)
                last.then_inc(s_fin_ev, 1)

            start = Batch(0, 0, 0)
            dve.wait_ge(s_const, 2)
            nc.vector.tensor_reduce(q_mask[:, :], head_rows[:, :, :], AX.X, ALU.add).then_inc(s_chain, 1)
            dve.wait_ge(s_chain, 1)
            nc.vector.tensor_scalar(q_mask[:, :], q_mask[:, :], -Q_SCALE / W_UP, None, ALU.mult).then_inc(s_qmask, 1)
            for k in range(NX):
                turn_lo(start, k, TURN_BANKS)
            def split_weight(n, lo, raw, hi):
                dve.wait_ge(s_wsplit_hi, n + 1)
                low_part(lo, raw, W_UP, hi).then_inc(s_wsplit_lo, 1)

            split_weight(0, wq_lo[:, :, :], wq_sb[:, :, :], wq_hi[:, :, :])
            split_weight(1, w_lo[:, :, 0, :], w_raw[:, :, 0, :], w_hi[:, :, 0, :])
            low_part(wk_last[:, :, 1, :], w_raw[:, :, 0, C - CR:C], W_UP, w_hi[:, :, 0, C - CR:C]).then_inc(s_wk_last, 1)
            make_lo(start, PIECE_Q, SETUP_BANKS)
            dve.wait_ge(s_prep_lo, PIECE_Q + 1)
            dve.wait_ge(s_const, 3)
            for dst, src in q_restack(0, (2, 3)):
                nc.vector.tensor_copy(dst, src).then_inc(s_qst[0], 16)
            dve.wait_ge(s_setup_pe, 1)
            nc.vector.tensor_copy(ip_T[:, :, :].rearrange("p e t -> p (e t)"), ps_val[:, 0:EC * 64]).then_inc(s_setup_ev, 1)
            for k in PIECES_K:
                make_lo(start, k, SETUP_BANKS)
            dve.wait_ge(s_setup_pe, 2)
            for m, c0, c1 in ((P, 0, CC - 1), (CR, CC - 1, CC)):
                last = nc.vector.tensor_copy(kip_hi[0:m, c0:c1, :, :].rearrange("p c n b -> p (c n b)"), ps_light[0:m, c0 * 64:c1 * 64])
            last.then_inc(s_setup_ev, 1)
            dve.wait_ge(s_setup_ev, 2)
            for m, c0, c1 in ((P, 0, CC - 1), (CR, CC - 1, CC)):
                last = nc.vector.tensor_tensor(kip_lo[0:m, c0:c1, :, :].rearrange("p c n b -> p (c n b)"), ps_light[0:m, c0 * 64:c1 * 64],
                                               kip_hi[0:m, c0:c1, :, :].rearrange("p c n b -> p (c n b)"), ALU.subtract)
            last.then_inc(s_setup_ev, 1)
            split_weight(2, w_lo[:, :, 1, :], w_raw[:, :, 1, :], w_hi[:, :, 1, :])
            dve.wait_ge(s_prep_lo, PIECES_K[-1] + 1)
            dve.wait_ge(s_kip, 1)
            for dst, src in k_restack(0, (3,)):
                nc.vector.tensor_copy(dst, src).then_inc(s_kst[0], 16)
            dve.wait_ge(s_ip, 16 * NIP)
            nc.vector.tensor_tensor_reduce(out=ip_sq[:, :], in0=ip_rows[:, :], in1=ip_rows[:, :], scale=1.0, scalar=0.0,
                                           op0=ALU.mult, op1=ALU.add, accum_out=ip_norm[:, 0:1]).then_inc(s_chain, 1)
            dve.wait_ge(s_chain, 2)
            nc.vector.tensor_scalar(ip_norm[:, 1:2], ip_norm[:, 0:1], EPS * EPS, None, ALU.max).then_inc(s_ipsq, 1)
            for k in PIECES_V[:2]:
                make_lo(start, k, SETUP_BANKS)
            dve.wait_ge(s_pool_set, 2)
            nc.vector.tensor_scalar(ip_norm[:, 3:4], ip_norm[:, 2:3], SEM_SCALE / G_DOWN, None, ALU.mult).then_inc(s_chain, 1)
            dve.wait_ge(s_chain, 3)
            nc.vector.tensor_scalar(ip_diag[:, :], ident[0:64, 0:64], ip_norm[:, 3:4], None, ALU.mult).then_inc(s_ipdiag, 1)
            for k in range(NX):
                turn_lo(Batch(1, 1, 0), k, TURN_BANKS)
            for k in PIECES_G:
                make_lo(start, k, SETUP_BANKS)
            dve.wait_ge(s_setup_pe, 3)
            nc.vector.tensor_copy(vip_rows[:, :], ps_val[0:64, 0:C]).then_inc(s_setup_ev, 1)
            dve.wait_ge(s_setup_pe, 4)
            nc.vector.tensor_copy(ip_inv[:, :, :].rearrange("s n b -> s (n b)"), ps_light[0:S, 0:64]).then_inc(s_setup_ev, 1)
            minimum(start, 0)
            minimum(start, 1)
            make_lo(start, NM - 1, SETUP_BANKS)
            probs_lo(start, 0)
            minimum(start, 2)
            split_weight(3, wo_lo[:, :, :], wo_sb[:, :, :], wo_hi[:, :, :])
            dve.wait_ge(s_small, 32)

            def body(b, prepare, turning, finishing):
                later = 0 if prepare else SOFT_LATER

                def softly(h, place):
                    if finishing and (h - later, place) in SOFT_AT:
                        soft(b.last(), SOFT_AT[h - later, place])

                for h in range(H):
                    if h + 3 < H:
                        minimum(b, h + 3)
                    elif prepare:
                        minimum(b.next(), h + 3 - H)
                    softly(h, 0)
                    if h + 1 < H:
                        probs_lo(b, h + 1)
                    elif prepare:
                        probs_lo(b.next(), 0)
                    if prepare and h - 1 in MAKE_STEP:
                        make_lo(b.next(), MAKE_STEP[h - 1])
                    if turning and h - 1 in TURN_STEP:
                        turn_lo(b.next().next(), TURN_STEP[h - 1])
                    if finishing and h - 1 in FINISH_STEP:
                        finish(b.last(), FINISH_STEP[h - 1])
                    softly(h, 1)
                    quadratic(b, h)
                    softly(h, 2)
                    if not prepare and h in AHEAD_NORM_STEPS:
                        norms_ahead(b, AHEAD_NORM_STEPS.index(h))

            def tail(b):
                for k in range(SOFT):
                    soft(b.last(), k, ahead=True)
                for k in range(NF):
                    finish(b.last(), k)

            all_batches(dve, body, tail)


_INS = ['x', 'ctx_2048', 'fside_S_0', 'L0_xattn_W_q', 'L0_xattn_W_k', 'L0_xattn_W_v', 'L0_xattn_W_k_ip', 'L0_xattn_W_v_ip',
        'L0_xattn_W_out', 'L0_xattn_b_out']


def kernel(**inputs):
    import numpy as np
    import concourse.bacc as bacc
    from concourse.bass_utils import run_bass_kernel_spmd

    nc = bacc.Bacc("TRN2", target_bir_lowering=False, num_devices=1)
    arrays, args = {}, []
    for name in _INS:
        a = np.ascontiguousarray(inputs[name])
        arrays[f"in_{name}"] = a
        args.append(nc.dram_tensor(f"in_{name}", a.shape, mybir.dt.from_np(a.dtype), kind="ExternalInput").ap())
    args.append(nc.dram_tensor("out_0", (B, S, C), F32, kind="ExternalOutput").ap())
    build(nc, *args)
    r = run_bass_kernel_spmd(nc, [arrays], core_ids=[0])
    return r.results[0]["out_0"]
```
